# Optimizing a Trainium2 kernel written in Bass

```python
import numpy as np
import jax
import jax.numpy as jnp

def _softmax(x, axis=-1):
    return jax.nn.softmax(x, axis=axis)

def _gelu(x):
    return jax.nn.gelu(x, approximate=True)

def _silu(x):
    return jax.nn.silu(x)

def _sigmoid(x):
    return jax.nn.sigmoid(x)

def _layernorm(x, axis=-1, eps=1e-05):
    m = jnp.mean(x, axis=axis, keepdims=True)
    v = jnp.var(x, axis=axis, keepdims=True)
    return (x - m) / jnp.sqrt(v + eps)

def _scatter_add(tgt, idx, src, axis=0):
    return tgt.at[idx].add(src)

def _segment_sum(src, seg, n):
    return jax.ops.segment_sum(src, seg, n)
kernel_name = 'mk_macaron_d1_jaxref_r8_9c23ff'

def setup_inputs(seed: int=0):
    np.random.seed(seed)
    _w = jnp.asarray

    def _L0_attn_setup():
        import jax, jax.numpy as jnp
        import numpy as np
        HIDDEN = 256
        NUM_HEADS = 16
        HEAD_SIZE = HIDDEN // NUM_HEADS
        SEQ = 256
        BATCH = 2

        def alibi_causal_bias(seq_len: int, num_heads: int) -> jnp.ndarray:
            i = jnp.arange(seq_len)[:, None]
            j = jnp.arange(seq_len)[None, :]
            dist = -(i - j).astype(jnp.float32)
            causal = jnp.where(j > i, -jnp.inf, 0.0)
            base = jnp.where(j > i, 0.0, dist) + causal
            if num_heads <= 8:
                slopes = jnp.asarray([1.0 / 2 ** k for k in range(num_heads)], jnp.float32)
            else:
                slopes = jnp.asarray([1.0 / 2 ** (k / 2) for k in range(num_heads)], jnp.float32)
            return slopes[None, :, None, None] * dist[None, None] * (j <= i)[None, None] + causal[None, None]
        key = jax.random.key(seed)
        ks = jax.random.split(key, 3)
        sd = 1.0 / np.sqrt(HIDDEN)
        return {'x': jax.random.normal(ks[0], (BATCH, SEQ, HIDDEN), jnp.float32), 'Wqkv': jax.random.normal(ks[1], (HIDDEN, 3 * HIDDEN), jnp.float32) * sd, 'bqkv': jnp.zeros((3 * HIDDEN,), jnp.float32), 'Wo': jax.random.normal(ks[2], (HIDDEN, HIDDEN), jnp.float32) * sd, 'bo': jnp.zeros((HIDDEN,), jnp.float32)}
    _L0_attn_in = _L0_attn_setup()

    def _L0_ffn_setup():
        import jax, jax.numpy as jnp
        import numpy as np
        ALPHA = 1.702
        LIMIT = 7.0
        EPS = 1e-05
        TOP_K = 4
        key = jax.random.key(seed)
        ks = jax.random.split(key, 8)
        B, S, H, I, E = (2, 64, 256, 256, 16)
        return {'x': jax.random.normal(ks[0], (B, S, H), jnp.float32), 'norm_w': jnp.ones((H,), jnp.float32), 'gate_w': jax.random.normal(ks[1], (E, H), jnp.float32) * 0.02, 'gate_b': jax.random.normal(ks[2], (E,), jnp.float32) * 0.02, 'w1': jax.random.normal(ks[3], (E, 2 * I, H), jnp.float32) * 0.02, 'b1': jax.random.normal(ks[4], (E, 2 * I), jnp.float32) * 0.02, 'w2': jax.random.normal(ks[5], (E, H, I), jnp.float32) * 0.02, 'b2': jax.random.normal(ks[6], (E, H), jnp.float32) * 0.02}
    _L0_ffn_in = _L0_ffn_setup()
    _d = {'L0_attn_x': _L0_attn_in['x'], 'L0_attn_Wqkv': _L0_attn_in['Wqkv'], 'L0_attn_bqkv': _L0_attn_in['bqkv'], 'L0_attn_Wo': _L0_attn_in['Wo'], 'L0_attn_bo': _L0_attn_in['bo'], 'L0_ffn_norm_w': _L0_ffn_in['norm_w'], 'L0_ffn_gate_w': _L0_ffn_in['gate_w'], 'L0_ffn_gate_b': _L0_ffn_in['gate_b'], 'L0_ffn_w1': _L0_ffn_in['w1'], 'L0_ffn_b1': _L0_ffn_in['b1'], 'L0_ffn_w2': _L0_ffn_in['w2'], 'L0_ffn_b2': _L0_ffn_in['b2']}
    _x0 = _d['L0_attn_x']
    _d['L0_attn_x'] = jax.random.normal(jax.random.fold_in(jax.random.key(seed), 1), (4, 512, 256), dtype=_x0.dtype)
    del _x0
    return _d

def reference(L0_attn_x, L0_attn_Wqkv, L0_attn_bqkv, L0_attn_Wo, L0_attn_bo, L0_ffn_norm_w, L0_ffn_gate_w, L0_ffn_gate_b, L0_ffn_w1, L0_ffn_b1, L0_ffn_w2, L0_ffn_b2):

    def _L0_attn_ref(x, Wqkv, bqkv, Wo, bo):
        import jax, jax.numpy as jnp
        import numpy as np
        HIDDEN = 256
        NUM_HEADS = 16
        HEAD_SIZE = HIDDEN // NUM_HEADS
        SEQ = 256
        BATCH = 2

        def alibi_causal_bias(seq_len: int, num_heads: int) -> jnp.ndarray:
            i = jnp.arange(seq_len)[:, None]
            j = jnp.arange(seq_len)[None, :]
            dist = -(i - j).astype(jnp.float32)
            causal = jnp.where(j > i, -jnp.inf, 0.0)
            base = jnp.where(j > i, 0.0, dist) + causal
            if num_heads <= 8:
                slopes = jnp.asarray([1.0 / 2 ** k for k in range(num_heads)], jnp.float32)
            else:
                slopes = jnp.asarray([1.0 / 2 ** (k / 2) for k in range(num_heads)], jnp.float32)
            return slopes[None, :, None, None] * dist[None, None] * (j <= i)[None, None] + causal[None, None]
        b, s, h = x.shape
        scale = 1.0 / np.sqrt(HEAD_SIZE)
        qkv = x @ Wqkv + bqkv
        q, k, v = jnp.split(qkv, 3, axis=-1)

        def heads(t):
            return t.reshape(b, s, NUM_HEADS, HEAD_SIZE).transpose(0, 2, 1, 3)
        q, k, v = (heads(q), heads(k), heads(v))
        scores = jnp.einsum('bhid,bhjd->bhij', q, k) * scale
        scores = scores + alibi_causal_bias(s, NUM_HEADS)
        attn = jax.nn.softmax(scores, axis=-1)
        out = jnp.einsum('bhij,bhjd->bhid', attn, v)
        out = out.transpose(0, 2, 1, 3).reshape(b, s, NUM_HEADS * HEAD_SIZE)
        return out @ Wo + bo

    def _L0_ffn_ref(x, norm_w, gate_w, gate_b, w1, b1, w2, b2):
        import jax, jax.numpy as jnp
        import numpy as np
        ALPHA = 1.702
        LIMIT = 7.0
        EPS = 1e-05
        TOP_K = 4
        B, S, H = x.shape
        M = B * S
        E = gate_w.shape[0]
        xf = x.reshape(M, H)
        t = xf * jax.lax.rsqrt(jnp.mean(xf * xf, axis=-1, keepdims=True) + EPS) * norm_w
        logits = t @ gate_w.T + gate_b
        vals, idx = jax.lax.top_k(logits, TOP_K)
        gates_k = jax.nn.softmax(vals, axis=-1)
        G = jnp.zeros((M, E), x.dtype).at[jnp.arange(M)[:, None], idx].set(gates_k)
        h = jnp.einsum('mh,eoh->emo', t, w1) + b1[:, None, :]
        a = jnp.minimum(h[..., ::2], LIMIT)
        b = jnp.clip(h[..., 1::2], -LIMIT, LIMIT)
        act = a * jax.nn.sigmoid(ALPHA * a) * (b + 1.0)
        y = jnp.einsum('emi,edi->emd', act, w2) + b2[:, None, :]
        delta = jnp.einsum('me,emd->md', G, y)
        return x + delta.reshape(B, S, H)
    x = L0_attn_x
    x = x + 0.5 * _L0_ffn_ref(_layernorm(x, axis=-1), L0_ffn_norm_w, L0_ffn_gate_w, L0_ffn_gate_b, L0_ffn_w1, L0_ffn_b1, L0_ffn_w2, L0_ffn_b2)
    x = x + _L0_attn_ref(_layernorm(x, axis=-1), L0_attn_Wqkv, L0_attn_bqkv, L0_attn_Wo, L0_attn_bo)
    x = x + 0.5 * _L0_ffn_ref(_layernorm(x, axis=-1), L0_ffn_norm_w, L0_ffn_gate_w, L0_ffn_gate_b, L0_ffn_w1, L0_ffn_b1, L0_ffn_w2, L0_ffn_b2)
    return x

_drawn_inputs = setup_inputs


def setup_inputs(seed=0):
    import zlib

    import numpy as np

    out = dict(_drawn_inputs(seed))
    spreads = {'L0_attn_bqkv': (0.0, 0.1), 'L0_attn_bo': (0.0, 0.1), 'L0_ffn_norm_w': (1.0, 0.6)}
    factors = {'L0_ffn_gate_w': 3.579,
     'L0_ffn_gate_b': 8.0,
     'L0_ffn_w1': 3.303,
     'L0_ffn_b1': 8.0,
     'L0_ffn_w2': 3.209,
     'L0_ffn_b2': 8.0}
    for name, (base, spread) in spreads.items():
        noise = np.random.default_rng([zlib.crc32(name.encode()), seed]).standard_normal(out[name].shape)
        drawn = base * np.exp(spread * noise) if base else spread * noise
        out[name] = jnp.asarray(drawn.astype(out[name].dtype))
    for name, factor in factors.items():
        out[name] = (out[name] * factor).astype(out[name].dtype)
    return out
```

```python
import concourse.bass as bass
from concourse import mybir
from contextlib import ExitStack

f32 = mybir.dt.float32
f16 = mybir.dt.float16
u32 = mybir.dt.uint32
i32 = mybir.dt.int32
ALU = mybir.AluOpType
ACT = mybir.ActivationFunctionType
AX = mybir.AxisListType

P = 128
B, SEQ, H = 4, 512, 256
T = B * SEQ
NT = T // P
TPB = SEQ // P
HC = H // P
E, K, INNER = 16, 4, 256
SLOTS = 80
HEADS, D = 16, 16
QG = HEADS * 32 // P
EPS = 1e-5
LIMIT = 7.0
TS = 2.0 ** 4
WS = 2.0 ** 6
S = TS * WS
MASKED = -1e30


def build(nc, x, wq, wk, wv, bq, bk, bv, wo, bo, norm_w, gate_w, gate_b, w1, b1, w2, b2, out):
    ctx = ExitStack()
    known = {}
    holds = nc.alloc_semaphore("holds")

    def sem(name):
        if name not in known:
            known[name] = nc.alloc_semaphore(name)
        return known[name]

    def end_phase():
        nc.clear_and_free_semaphores(list(known.values()))
        known.clear()
        nc.all_engine_barrier()

    def keep(name, shape, dt=f32):
        return ctx.enter_context(nc.sbuf_tensor(name, shape, dt))

    def spread(vector, n=P):
        return vector.rearrange("(a n) -> a n", a=1).broadcast_to([n, vector.shape[0]])

    def chained(eng, s, start=0):
        count = [start]

        def step(instruction):
            count[0] += 1
            instruction.then_inc(s, 1)
            eng.wait_ge(s, count[0])
        return step

    def hold(eng):
        eng.sem_inc(holds, 1)

    def rounds(eng, count, emit):
        emit(0)
        with eng.Fori(1, count) as i:
            emit(i)

    def later(n, first):
        return not isinstance(n, int) or n >= first

    def rsqrt(dve, step, out_, var, shifted, root, newton, to_root, rooted, value):
        dve.tensor_scalar(shifted, var, EPS, None, ALU.add).then_inc(to_root, 1)
        dve.wait_ge(rooted, value)
        step(dve.reciprocal(out_, root))
        step(dve.tensor_tensor(newton, out_, out_, ALU.mult))
        step(dve.tensor_tensor(newton, newton, shifted, ALU.mult))
        step(dve.tensor_scalar(newton, newton, -0.5, 1.5, ALU.mult, ALU.add))
        step(dve.tensor_tensor(out_, out_, newton, ALU.mult))

    with ctx:
        t_rows = [nc.dram_tensor(f"t_rows{m}", (T, 2 * H), f16, kind="Internal").ap() for m in range(2)]
        sums = [[nc.dram_tensor(f"sums{m}_{j}", (T + P, H), f32, kind="Internal").ap() for j in range(2)]
                for m in range(2)]
        bias_dram = nc.dram_tensor("bias_split", (2, E, 2 * INNER), f16, kind="Internal").ap()

        X = keep("X", [P, NT, H])
        w1s = keep("w1s", [P, E, HC, 2, 2 * INNER], f16)
        w2s = keep("w2s", [P, E, 2, 2, H], f16)
        b1s = keep("b1s", [P, E, 2 * INNER], f16)
        ones16 = keep("ones16", [P, P], f16)
        ident = keep("ident", [P, P])
        ident16 = keep("ident16", [P, P], f16)
        before = keep("before", [P, P], f16)
        normw = keep("normw", [P, H])
        gatew = keep("gatew", [P, HC, E])
        gateb = keep("gateb", [P, E])
        b2r = keep("b2r", [E, H])
        iota_e = keep("iota_e", [P, E])
        iota_t = keep("iota_t", [P, SLOTS])
        iota_p = keep("iota_p", [P, P])
        tok = keep("tok", [P, NT])
        idle = keep("idle", [P, 1])
        bank = [ctx.enter_context(nc.psum_tensor(f"bank{i}", [P, 512], f32)) for i in range(8)]
        bank16 = [b[:, :].bitcast(f16) for b in bank]

        def setup():
            with ExitStack() as own:
                N1, N2 = HC * 2 * INNER, 2 * H
                stage = [own.enter_context(nc.sbuf_tensor(f"stage{j}", [P, N1 + N2], f32)) for j in range(2)]
                b1_raw = own.enter_context(nc.sbuf_tensor("b1_raw", [E, 2 * INNER], f32))
                b1_hi = own.enter_context(nc.sbuf_tensor("b1_hi", [E, 2 * INNER], f16))
                b1_lo = own.enter_context(nc.sbuf_tensor("b1_lo", [E, 2 * INNER], f16))
                loaded = [sem("weights_loaded0"), sem("weights_loaded1")]
                view1 = lambda j: stage[j][:, 0:N1].rearrange("p (e k n) -> p e k n", e=1, k=HC)
                view2 = lambda j: stage[j][:, N1:].rearrange("p (e k n) -> p e k n", e=1, k=2)
                block = own.enter_context(nc.Block())

                @block.sync
                def _(sp):
                    sp.dma_start(b1_raw[:, :], b1).then_inc(sem("b1_loaded"), 16)
                    for dst, src in ((normw[:, :], spread(norm_w)), (gateb[:, :], spread(gate_b)),
                                     (gatew[:, :, :], gate_w), (b2r[:, :], b2),
                                     (X[:, :, :], x.rearrange("(t p) h -> p t h", p=P))):
                        sp.dma_start(dst, src).then_inc(sem("inputs_loaded"), 16)
                    with sp.Fori(0, E // 2) as i:
                        for j in range(2):
                            sp.dma_start(stage[j][:, 0:N1], w1[bass.ds(i * 2 + j, 1)].rearrange("e p n -> p (e n)"))\
                              .then_inc(loaded[j], 16)
                            sp.dma_start(stage[j][:, N1:], w2[bass.ds(i * 2 + j, 1)].rearrange("e p n -> p (e n)"))\
                              .then_inc(loaded[j], 16)
                        sp.wait_ge(sem("lo_split"), i * 2 + 2)
                        hold(sp)
                    sp.wait_ge(sem("b1_split"), 2)
                    sp.dma_start(bias_dram[0], b1_hi[:, :]).then_inc(sem("b1_stored"), 16)
                    sp.dma_start(bias_dram[1], b1_lo[:, :]).then_inc(sem("b1_stored"), 16)
                    sp.wait_ge(sem("b1_stored"), 32)
                    sp.wait_ge(sem("b1_zeroed"), 1)
                    sp.dma_start(b1s[0:2, :, :], bias_dram).then_inc(sem("inputs_loaded"), 16)
                    sp.wait_ge(sem("inputs_loaded"), 16 * 6)

                @block.scalar
                def _(act):
                    act.wait_ge(sem("b1_loaded"), 16)
                    act.activation(b1_hi[:, :], b1_raw[:, :], ACT.Copy, scale=S).then_inc(sem("b1_split"), 1)
                    with act.Fori(0, E // 2) as i:
                        for j in range(2):
                            e = bass.ds(i * 2 + j, 1)
                            act.wait_ge(loaded[j], i * 32 + 32)
                            act.activation(w1s[:, e, :, 0, :], view1(j), ACT.Copy, scale=WS)
                            act.activation(w2s[:, e, :, 0, :], view2(j), ACT.Copy, scale=WS)\
                               .then_inc(sem("hi_split"), 1)

                @block.vector
                def _(dve):
                    dve.wait_ge(sem("b1_split"), 1)
                    dve.scalar_tensor_tensor(b1_lo[:, :], b1_raw[:, :], S, b1_hi[:, :], ALU.mult, ALU.subtract)\
                       .then_inc(sem("b1_split"), 1)
                    with dve.Fori(0, E // 2) as i:
                        for j in range(2):
                            e = bass.ds(i * 2 + j, 1)
                            dve.wait_ge(sem("hi_split"), i * 2 + j + 1)
                            dve.scalar_tensor_tensor(w1s[:, e, :, 1, :], view1(j), WS, w1s[:, e, :, 0, :],
                                                     ALU.mult, ALU.subtract)
                            dve.scalar_tensor_tensor(w2s[:, e, :, 1, :], view2(j), WS, w2s[:, e, :, 0, :],
                                                     ALU.mult, ALU.subtract).then_inc(sem("lo_split"), 1)

                @block.gpsimd
                def _(pool):
                    made = sem("constants")
                    pool.memset(b1s[:, :, :], 0.0).then_inc(sem("b1_zeroed"), 1)
                    pool.memset(ones16[:, :], 1.0).then_inc(made, 1)
                    pool.memset(ident[:, :], 0.0).then_inc(made, 1)
                    pool.memset(ident16[:, :], 0.0).then_inc(made, 1)
                    for dst, step, base, per_partition in ((iota_e, 1, 0, 0), (iota_t, 1, 0, 0), (iota_p, 1, 0, 0),
                                                           (tok, P, 1, 1), (idle, 1, T + 1, 1)):
                        pool.iota(dst[:, :], [[step, dst.shape[1]]], base, per_partition,
                                  allow_small_or_imprecise_dtypes=True).then_inc(made, 1)
                    pool.wait_ge(made, 8)
                    for square in (ident, ident16):
                        pool.affine_select(square[:, :], square[:, :], [[-1, P]], ALU.not_equal, 1.0, 0, 1)\
                            .then_inc(made, 1)
                    pool.affine_select(before[:, :], ones16[:, :], [[1, P]], ALU.is_gt, 0.0, 0, -1)\
                        .then_inc(made, 1)

        def route(m, gather_at, add_at, gate_at, expert_at):
            with ExitStack() as own:
                def tmp(name, shape, dt=f32):
                    return own.enter_context(nc.sbuf_tensor(f"{name}_r{m}", shape, dt))
                ev = lambda name: sem(f"{name}_{m}")
                NB = 2
                stats = tmp("stats", [P, NT, 6])
                mv = tmp("mv", [P, NT, 2])
                rz = tmp("rz", [P, NT])
                rt = tmp("rt", [P, NT])
                shifted = tmp("shifted", [P, NT])
                root = tmp("root", [P, NT])
                newton = tmp("newton", [P, NT])
                meansq = tmp("meansq", [P, NT])
                z = tmp("z", [P, NB, H])
                t = tmp("t", [P, NB, H])
                row = tmp("row", [P, NB, 2 * H], f16)
                tT = tmp("tT", [P, NB, HC, P])
                logits = tmp("logits", [P, NT, E])
                row_stored = [ev(f"row_stored{j}") for j in range(NB)]

                with nc.Block() as block:
                    @block.vector
                    def _(dve):
                        for i in range(NT):
                            dve.bn_stats(stats[:, i, :], X[:, i, :]).then_inc(ev("stats"), 1)
                        for i in range(NT):
                            dve.wait_ge(ev("stats"), i + 1)
                            dve.bn_aggr(mv[:, i, :], stats[:, i, :]).then_inc(ev("moments"), 1)
                        dve.wait_ge(ev("moments"), NT)
                        step = chained(dve, ev("scales"))
                        rsqrt(dve, step, rz[:, :], mv[:, :, 1], shifted[:, :], root[:, :], newton[:, :],
                              ev("to_root"), ev("rooted"), 1)
                        step(dve.tensor_tensor(rt[:, :], rz[:, :], rz[:, :], ALU.mult))
                        step(dve.tensor_tensor(meansq[:, :], rt[:, :], mv[:, :, 1], ALU.mult))
                        rsqrt(dve, step, rt[:, :], meansq[:, :], shifted[:, :], root[:, :], newton[:, :],
                              ev("to_root"), ev("rooted"), 2)
                        step(dve.tensor_scalar(rt[:, :], rt[:, :], TS, None, ALU.mult))
                        with dve.Fori(0, NT // NB) as i:
                            for j in range(NB):
                                n = i * NB + j
                                one = bass.ds(n, 1)
                                dve.tensor_scalar(z[:, j:j + 1, :], X[:, one, :], mv[:, one, 0], rz[:, one],
                                                  ALU.subtract, ALU.mult).then_inc(ev("z"), 1)
                                dve.wait_ge(ev("z"), n + 1)
                                dve.scalar_tensor_tensor(t[:, j, :], z[:, j, :], rt[:, one], normw[:, :],
                                                         ALU.mult, ALU.mult).then_inc(ev("t"), 1)
                                dve.wait_ge(ev("row_hi"), n + 1)
                                dve.tensor_tensor(row[:, j, H:], t[:, j, :], row[:, j, 0:H], ALU.subtract)\
                                   .then_inc(ev("row_lo"), 1)
                                dve.wait_ge(ev("gate_product"), n + 1)
                                dve.scalar_tensor_tensor(
                                    logits[:, one, :], bank[2 + j][:, 0:E].rearrange("p (o e) -> p o e", o=1), 1.0 / TS,
                                    gateb[:, :].rearrange("p (o e) -> p o e", o=1), ALU.mult, ALU.add)\
                                   .then_inc(ev("logits"), 1)

                    @block.scalar
                    def _(act):
                        for n in range(2):
                            act.wait_ge(ev("to_root"), n + 1)
                            act.activation(root[:, :], shifted[:, :], ACT.Sqrt).then_inc(ev("rooted"), 1)
                        def emit(i):
                            for j in range(NB):
                                n = i * NB + j
                                if later(i, 1):
                                    act.wait_ge(row_stored[j], i * 16)
                                act.wait_ge(ev("t"), n + 1)
                                act.activation(row[:, j, 0:H], t[:, j, :], ACT.Copy).then_inc(ev("row_hi"), 1)
                                act.wait_ge(ev("t_turned"), n + 1)
                                act.activation(tT[:, j], bank[j][:, 0:H].rearrange("p (k n) -> p k n", k=HC),
                                               ACT.Copy).then_inc(ev("tT"), 1)
                        rounds(act, NT // NB, emit)

                    @block.tensor
                    def _(pe):
                        with pe.Fori(0, NT // NB) as i:
                            for j in range(NB):
                                n = i * NB + j
                                pe.wait_ge(ev("t"), n + 1)
                                for k in range(HC):
                                    mm = pe.transpose(bank[j][:, k * P:(k + 1) * P], t[:, j, k * P:(k + 1) * P],
                                                      ident[:, :])
                                mm.then_inc(ev("t_turned"), 1)
                                pe.wait_ge(ev("tT"), n + 1)
                                for k in range(HC):
                                    mm = pe.matmul(bank[2 + j][:, 0:E], tT[:, j, k, :], gatew[:, k, :],
                                                   start=(k == 0), stop=(k == HC - 1))
                                mm.then_inc(ev("gate_product"), 1)

                    @block.sync
                    def _(sp):
                        with sp.Fori(0, NT // NB) as i:
                            for j in range(NB):
                                n = i * NB + j
                                sp.wait_ge(ev("row_lo"), n + 1)
                                sp.dma_start(t_rows[m][bass.ds(n * P, P), :], row[:, j, :]).then_inc(row_stored[j], 16)
                        for j in range(NB):
                            sp.wait_ge(row_stored[j], 16 * NT // NB)

                top = tmp("top", [P, NT, 8])
                topi = tmp("topi", [P, NT, 8], u32)
                topf = tmp("topf", [P, NT, K])
                ex = tmp("ex", [P, NT, K])
                total = tmp("total", [P, NT])
                gate = tmp("gate", [P, NT, K])
                chosen = tmp("chosen", [P, NT, K, E])
                work = tmp("work", [P, NT, K, E])
                mask16 = tmp("mask16", [P, NT, E], f16)
                gates = tmp("gates", [P, NT, E])
                count = tmp("count", [P, E], i32)
                tiles = tmp("tiles", [P, E])
                end = tmp("end", [P, E])
                ones_e = tmp("ones_e", [P, E])
                pos = tmp("pos", [P, NT, E])
                slot = tmp("slot", [P, NT, K], i32)
                slot_low = tmp("slot_low", [P, NT, K], i32)
                slot_f = tmp("slot_f", [P, NT, K])
                slot_row = tmp("slot_row", [P, NT, K])
                slot_tile = tmp("slot_tile", [P, NT, K])
                passed = tmp("passed", [P, SLOTS, E])
                expert_f = tmp("expert_f", [P, SLOTS])
                hot_row = tmp("hot_row", [P, K, P])
                hot_tile = tmp("hot_tile", [P, K, 2, SLOTS])
                zeros = tmp("zeros", [P, 2 * SLOTS])
                gT = tmp("gT", [E, T])
                idles = tmp("idles", [P, SLOTS])
                table = tmp("table", [P, 2, SLOTS])
                first = tmp("first", [P, 2, H])
                first_stored = [ev("first_stored0"), ev("first_stored1")]
                zero_sum = tmp("zero_sum", [P, H])

                with nc.Block() as block:
                    @block.vector
                    def _(dve):
                        dve.memset(zeros[:, :], 0.0).then_inc(ev("zeroed"), 1)
                        dve.memset(zero_sum[:, :], 0.0).then_inc(ev("zeroed"), 1)
                        dve.memset(ones_e[:, :], 1.0).then_inc(ev("zeroed"), 1)
                        dve.wait_ge(ev("zeroed"), 3)
                        for i in range(NT):
                            dve.max(top[:, i, :], logits[:, i, :]).then_inc(ev("top"), 1)
                        for i in range(NT):
                            dve.wait_ge(ev("top"), i + 1)
                            dve.max_index(topi[:, i, :], top[:, i, :], logits[:, i, :]).then_inc(ev("topi"), 1)
                        dve.tensor_tensor(ex[:, :, :], top[:, :, 0:K], top[:, :, 0:1].broadcast_to([P, NT, K]),
                                          ALU.subtract).then_inc(ev("shifted"), 1)
                        dve.wait_ge(ev("topi"), NT)
                        step = chained(dve, ev("route_steps"))
                        step(dve.tensor_copy(topf[:, :, :], topi[:, :, 0:K]))
                        step(dve.tensor_tensor(chosen[:, :, :, :],
                                               topf[:, :, :].unsqueeze(3).broadcast_to([P, NT, K, E]),
                                               iota_e[:, :].unsqueeze(1).unsqueeze(1).broadcast_to([P, NT, K, E]),
                                               ALU.is_equal))
                        with nc.allow_low_precision("zeros and ones"):
                            dve.tensor_reduce(mask16[:, :, :], chosen[:, :, :, :].rearrange("p t k e -> p t e k"),
                                              AX.X, ALU.add).then_inc(ev("mask"), 1)
                        dve.wait_ge(ev("exps"), 1)
                        step(dve.tensor_reduce(total[:, :], ex[:, :, :], AX.X, ALU.add))
                        step(dve.reciprocal(total[:, :], total[:, :]))
                        step(dve.tensor_tensor(gate[:, :, :], ex[:, :, :],
                                               total[:, :].unsqueeze(2).broadcast_to([P, NT, K]), ALU.mult))
                        step(dve.tensor_tensor(work[:, :, :, :], chosen[:, :, :, :],
                                               gate[:, :, :].unsqueeze(3).broadcast_to([P, NT, K, E]), ALU.mult))
                        dve.tensor_reduce(gates[:, :, :], work[:, :, :, :].rearrange("p t k e -> p t e k"),
                                          AX.X, ALU.add).then_inc(ev("gates"), 1)
                        dve.wait_ge(ev("gates"), 1)
                        dve.wait_ge(ev("ranks"), 1)
                        step(dve.tensor_scalar(count[:, :], bank[1][:, 0:E], P - 1.0, None, ALU.add))
                        step(dve.tensor_scalar(count[:, :], count[:, :], 7, None, ALU.arith_shift_right))
                        step(dve.tensor_copy(tiles[:, :], count[:, :]))
                        step(dve.tensor_tensor_scan(end[:, :], ones_e[:, :], tiles[:, :], 0.0, ALU.mult, ALU.add))
                        step(dve.tensor_tensor(tiles[:, :], end[:, :], tiles[:, :], ALU.subtract))
                        step(dve.tensor_scalar(tiles[:, :], tiles[:, :], float(P), None, ALU.mult))
                        step(dve.tensor_tensor(pos[:, :, :], bank[0][:, 0:NT * E].rearrange("p (t e) -> p t e", e=E),
                                               tiles[:, :].unsqueeze(1).broadcast_to([P, NT, E]), ALU.add))
                        step(dve.tensor_tensor(work[:, :, :, :], chosen[:, :, :, :],
                                               pos[:, :, :].unsqueeze(2).broadcast_to([P, NT, K, E]), ALU.mult))
                        step(dve.tensor_reduce(slot_f[:, :, :], work[:, :, :, :], AX.X, ALU.add))
                        step(dve.tensor_copy(slot[:, :, :], slot_f[:, :, :]))
                        step(dve.tensor_scalar(slot_low[:, :, :], slot[:, :, :], P - 1, None, ALU.bitwise_and))
                        step(dve.tensor_scalar(slot[:, :, :], slot[:, :, :], 7, None, ALU.arith_shift_right))
                        step(dve.tensor_copy(slot_row[:, :, :], slot_low[:, :, :]))
                        step(dve.tensor_copy(slot_tile[:, :, :], slot[:, :, :]))
                        def place(i):
                            one = bass.ds(i, 1)
                            for k in range(K):
                                if later(i, 1):
                                    dve.wait_ge(ev("placed"), i * K + (k + 1 - K))
                                dve.tensor_scalar(hot_row[:, k, :], iota_p[:, :], slot_row[:, one, k], None,
                                                  ALU.is_equal)
                                dve.tensor_scalar(hot_tile[:, k, 0, :], iota_t[:, :], slot_tile[:, one, k],
                                                  tok[:, one], ALU.is_equal, ALU.mult)
                                dve.tensor_scalar(hot_tile[:, k, 1, :], iota_t[:, :], slot_tile[:, one, k],
                                                  gate[:, one, k], ALU.is_equal, ALU.mult).then_inc(ev("hots"), 1)
                        rounds(dve, NT, place)
                        step(dve.tensor_tensor(passed[:, :, :], end[:, :].unsqueeze(1).broadcast_to([P, SLOTS, E]),
                                               iota_t[:, :].unsqueeze(2).broadcast_to([P, SLOTS, E]), ALU.is_le))
                        step(dve.tensor_reduce(expert_f[:, :], passed[:, :, :], AX.X, ALU.add))
                        step(dve.tensor_scalar(expert_at[:, :], expert_f[:, :], E - 1.0, None, ALU.min))
                        dve.wait_ge(ev("placed_all"), 1)
                        step(dve.tensor_copy(table[:, :, :], bank[2][:, 0:2 * SLOTS].rearrange("p (a s) -> p a s", a=2)))
                        step(dve.tensor_scalar(gather_at[:, :], table[:, 0, :], -1.0, 0.0, ALU.add, ALU.max))
                        step(dve.tensor_scalar(idles[:, :], table[:, 0, :], 0.0, idle[:, 0:1], ALU.is_equal, ALU.mult))
                        step(dve.scalar_tensor_tensor(add_at[:, :], table[:, 0, :], -1.0, idles[:, :],
                                                      ALU.add, ALU.add))
                        step(dve.tensor_scalar(gate_at[:, :], table[:, 1, :], 1.0 / (S * WS), None, ALU.mult))
                        def start_sums(i):
                            for j in range(2):
                                n = i * 2 + j
                                one = bass.ds(n, 1)
                                if later(i, 1):
                                    dve.wait_ge(first_stored[j], i * 16)
                                dve.tensor_scalar(z[:, j:j + 1, :], X[:, one, :], mv[:, one, 0], rz[:, one],
                                                  ALU.subtract, ALU.mult).then_inc(ev("z_again"), 1)
                                dve.wait_ge(ev("z_again"), n + 1)
                                dve.wait_ge(ev("bias_product"), n + 1)
                                dve.tensor_tensor(first[:, j, :], z[:, j, :], bank[5 + j][:, 0:H], ALU.add)\
                                   .then_inc(ev("first"), 1)
                        rounds(dve, NT // 2, start_sums)

                    @block.scalar
                    def _(act):
                        act.wait_ge(ev("shifted"), 1)
                        act.activation(ex[:, :, :], ex[:, :, :], ACT.Exp).then_inc(ev("exps"), 1)
                        for g in range(NT // 4):
                            act.wait_ge(ev("gates_turned"), g + 1)
                            act.activation(gT[:, g * 512:(g + 1) * 512], bank[3 + g % 2][0:E, :], ACT.Copy)\
                               .then_inc(ev("gT"), 1)

                    @block.tensor
                    def _(pe):
                        pe.wait_ge(ev("mask"), 1)
                        flat = mask16[:, :, :].rearrange("p t e -> p (t e)")
                        for i in range(NT - 1):
                            later = NT - 1 - i
                            pe.matmul(bank[0][:, (i + 1) * E:NT * E].rearrange("p (t e) -> p t e", e=E), ones16[:, :],
                                      mask16[:, i:i + 1, :].broadcast_to([P, later, E]), start=(i == 0),
                                      stop=False, skip_group_check=True)
                        pe.matmul(bank[0][:, 0:NT * E], before[:, :], flat, start=False, stop=True,
                                  skip_group_check=True)
                        for i in range(NT):
                            mm = pe.matmul(bank[1][:, 0:E], ones16[:, :], mask16[:, i, :], start=(i == 0),
                                           stop=(i == NT - 1))
                        mm.then_inc(ev("ranks"), 1)
                        pe.wait_ge(ev("gates"), 1)
                        for g in range(NT // 4):
                            if g >= 2:
                                pe.wait_ge(ev("gT"), g - 1)
                            for c in range(4):
                                mm = pe.transpose(bank[3 + g % 2][0:E, c * P:(c + 1) * P], gates[:, 4 * g + c, :],
                                                  ident[:, :])
                            mm.then_inc(ev("gates_turned"), 1)
                        pe.wait_ge(ev("zeroed"), 3)
                        pe.matmul(bank[2][:, 0:2 * SLOTS], zeros[:, 0:P], zeros[:, :], start=True, stop=False,
                                  skip_group_check=True)
                        with pe.Fori(0, NT) as i:
                            for k in range(K):
                                pe.wait_ge(ev("hots"), i * K + k + 1)
                                pe.matmul(bank[2][:, 0:2 * SLOTS], hot_row[:, k, :],
                                          hot_tile[:, k].rearrange("p a s -> p (a s)"), start=False,
                                          stop=False, skip_group_check=True).then_inc(ev("placed"), 1)
                        pe.matmul(bank[2][:, 0:2 * SLOTS], zeros[:, 0:P], zeros[:, :], start=False, stop=True,
                                  skip_group_check=True).then_inc(ev("placed_all"), 1)
                        for n in range(NT):
                            if n % 4 == 0:
                                pe.wait_ge(ev("gT"), n // 4 + 1)
                            if n >= 2:
                                pe.wait_ge(ev("first"), n - 1)
                            pe.matmul(bank[5 + n % 2][:, 0:H], gT[:, n * P:(n + 1) * P], b2r[:, :], start=True,
                                      stop=True).then_inc(ev("bias_product"), 1)

                    @block.sync
                    def _(sp):
                        sp.wait_ge(ev("zeroed"), 3)
                        sp.dma_start(sums[m][0][T:T + P, :], zero_sum[:, :]).then_inc(ev("sums_zeroed"), 16)
                        with sp.Fori(0, NT + 1) as i:
                            sp.dma_start(sums[m][1][bass.ds(i * P, P), :], zero_sum[:, :])\
                              .then_inc(ev("sums_zeroed"), 16)
                        with sp.Fori(0, NT // 2) as i:
                            for j in range(2):
                                n = i * 2 + j
                                sp.wait_ge(ev("first"), n + 1)
                                sp.dma_start(sums[m][0][bass.ds(n * P, P), :], first[:, j, :])\
                                  .then_inc(first_stored[j], 16)
                        sp.wait_ge(ev("sums_zeroed"), 16 * (NT + 2))
                        for j in range(2):
                            sp.wait_ge(first_stored[j], 16 * NT // 2)

        def experts(m, gather_at, add_at, gate_at, expert_at):
            with ExitStack() as own:
                def tmp(name, shape, dt=f32):
                    return own.enter_context(nc.sbuf_tensor(f"{name}_x{m}", shape, dt))
                ev = lambda name: sem(f"{name}_{m}")
                NG = 4
                gidx = tmp("gidx", [P, NG, 1], u32)
                aidx = tmp("aidx", [P, 2, 1], u32)
                rows = tmp("rows", [P, NG, 2 * H], f16)
                rT = tmp("rT", [P, 2, 4, P], f16)
                a = tmp("a", [P, 2, INNER])
                b = tmp("b", [P, 2, INNER])
                p = tmp("p", [P, 2, INNER])
                h = tmp("h", [P, 2, INNER])
                hs = tmp("hs", [P, 2, 4, P], f16)
                hT = tmp("hT", [P, 2, 4, P], f16)
                y = tmp("y", [P, 2, H])
                gathered = [ev(f"gathered{j}") for j in range(NG)]
                added = [ev(f"added{j}") for j in range(2)]
                PRODUCTS = ((0, 0), (0, 1), (1, 0))

                def there(s, lag):
                    return not isinstance(s, int) or 0 <= s + lag < SLOTS

                with nc.Block() as block:
                    @block.gpsimd
                    def _(pool):
                        def gather(n, c):
                            if later(n, NG):
                                pool.wait_ge(ev("turned"), n - (NG - 1))
                            pool.tensor_copy(gidx[:, c, :], gather_at[:, bass.ds(n, 1)]).then_inc(ev("gidx"), 1)
                            pool.wait_ge(ev("gidx"), n + 1)
                            hold(pool)
                            pool.indirect_dma_start(rows[:, c, :], None, t_rows[m],
                                                    bass.IndirectOffsetOnAxis(ap=gidx[:, c, :], axis=0))\
                                .then_inc(gathered[c], 16)

                        def add(n, c, past):
                            if later(n, 2):
                                pool.wait_ge(added[c % 2], past * 16)
                            pool.tensor_copy(aidx[:, c % 2, :], add_at[:, bass.ds(n, 1)]).then_inc(ev("aidx"), 1)
                            pool.wait_ge(ev("y"), n + 1)
                            pool.wait_ge(ev("aidx"), n + 1)
                            hold(pool)
                            pool.indirect_dma_start(sums[m][c % 2],
                                                    bass.IndirectOffsetOnAxis(ap=aidx[:, c % 2, :], axis=0),
                                                    y[:, c % 2, :], None, compute_op=ALU.add)\
                                .then_inc(added[c % 2], 16)

                        for n in range(NG):
                            gather(n, n)
                        for n in range(4, 6):
                            gather(n, n % 4)
                        for n in range(4):
                            add(n, n, n // 2)
                            gather(n + 6, (n + 6) % 4)
                        with pool.Fori(1, (SLOTS - 8) // 4) as i:
                            for c in range(4):
                                add(i * 4 + c, c, i * 2 + c // 2)
                                gather(i * 4 + (c + 6), (c + 6) % 4)
                        for n in range(SLOTS - 8, SLOTS):
                            add(n, n % 4, n // 2)
                            if n + 6 < SLOTS:
                                gather(n + 6, (n + 6) % 4)
                        for j in range(2):
                            pool.wait_ge(added[j], 16 * SLOTS // 2)

                    @block.tensor
                    def _(pe):
                        def turn_rows(n, c, nth):
                            pe.wait_ge(gathered[c], nth * 16 + 16)
                            if later(n, 2):
                                pe.wait_ge(ev("rT"), n - 1)
                            for q in range(4):
                                mm = pe.transpose(bank16[c % 2][:, q * P:(q + 1) * P], rows[:, c, q * P:(q + 1) * P],
                                                  ident16[:, :])
                            mm.then_inc(ev("turned"), 1)

                        def expert(n):
                            return pe.value_load(expert_at[0:1, bass.ds(n, 1)], min_val=0, max_val=E - 1)

                        def up(n, c):
                            e = bass.ds(expert(n), 1)
                            pe.wait_ge(ev("rT"), n + 1)
                            if later(n, 2):
                                pe.wait_ge(ev("a"), n - 1)
                                pe.wait_ge(ev("b"), n - 1)
                            o = bank[2 + c % 2][:, :]
                            pe.matmul(o, ones16[:, :], b1s[:, e, :], start=True, stop=False)
                            for k in range(HC):
                                for r, w in PRODUCTS:
                                    mm = pe.matmul(o, rT[:, c % 2, 2 * r + k, :], w1s[:, e, k, w, :], start=False,
                                                   stop=(k == HC - 1 and r == 1))
                            mm.then_inc(ev("up"), 1)

                        def turn_h(n, c):
                            pe.wait_ge(ev("h_lo"), n + 1)
                            if later(n, 2):
                                pe.wait_ge(ev("hT"), n - 1)
                            for q in range(4):
                                mm = pe.transpose(bank16[4 + c % 2][:, q * P:(q + 1) * P], hs[:, c % 2, q, :],
                                                  ident16[:, :])
                            mm.then_inc(ev("h_turned"), 1)

                        def down(n, c):
                            e = bass.ds(expert(n), 1)
                            pe.wait_ge(ev("hT"), n + 1)
                            if later(n, 2):
                                pe.wait_ge(ev("y"), n - 1)
                            o = bank[6 + c % 2][:, 0:H]
                            for k in range(2):
                                for r, w in PRODUCTS:
                                    mm = pe.matmul(o, hT[:, c % 2, 2 * r + k, :], w2s[:, e, k, w, :],
                                                   start=(k == 0 and r == 0 and w == 0), stop=(k == 1 and r == 1))
                            mm.then_inc(ev("down"), 1)

                        def emit(s, c, nth):
                            if there(s, 1):
                                turn_rows(s + 1, (c + 1) % 4, nth)
                            if there(s, 0):
                                up(s, c)
                            if there(s, -2):
                                down(s - 2, (c - 2) % 4)
                            if there(s, -1):
                                turn_h(s - 1, (c - 1) % 4)

                        for s in range(-1, 4):
                            emit(s, s % 4, (s + 1) // 4)
                        with pe.Fori(1, (SLOTS - 4) // 4) as i:
                            for q in range(4):
                                emit(i * 4 + q, q, i + (q + 1) // 4)
                        for s in range(SLOTS - 4, SLOTS + 2):
                            emit(s, s % 4, (s + 1) // 4)

                    @block.scalar
                    def _(act):
                        def rows_out(n, c):
                            act.wait_ge(ev("turned"), n + 1)
                            if later(n, 2):
                                act.wait_ge(ev("up"), n - 1)
                            act.activation(rT[:, c % 2], bank16[c % 2][:, 0:512].rearrange("p (q n) -> p q n", q=4),
                                           ACT.Copy).then_inc(ev("rT"), 1)

                        def gelu(n, c):
                            act.wait_ge(ev("a"), n + 1)
                            if later(n, 2):
                                act.wait_ge(ev("h"), n - 1)
                            act.activation(p[:, c % 2, :], a[:, c % 2, :], ACT.Gelu_apprx_sigmoid, scale=1.0 / S)\
                               .then_inc(ev("p"), 1)

                        def h_hi(n, c):
                            act.wait_ge(ev("h"), n + 1)
                            if later(n, 2):
                                act.wait_ge(ev("h_turned"), n - 1)
                            act.activation(hs[:, c % 2, 0:2, :], h[:, c % 2, :].rearrange("p (k n) -> p k n", k=2),
                                           ACT.Copy).then_inc(ev("h_hi"), 1)

                        def y_out(n, c, past):
                            act.wait_ge(ev("down"), n + 1)
                            if later(n, 2):
                                act.wait_ge(added[c % 2], past * 16)
                            act.activation(y[:, c % 2, :], bank[6 + c % 2][:, 0:H], ACT.Copy,
                                           scale=gate_at[:, bass.ds(n, 1)]).then_inc(ev("y"), 1)

                        def emit(s, c, past):
                            if there(s, 0):
                                gelu(s, c)
                            if there(s, -2):
                                y_out(s - 2, (c - 2) % 4, past)
                            if there(s, 0):
                                h_hi(s, c)
                            if there(s, 2):
                                rows_out(s + 2, (c + 2) % 4)

                        for s in range(-2, 4):
                            emit(s, s % 4, (s - 2) // 2)
                        with act.Fori(1, (SLOTS - 4) // 4) as i:
                            for q in range(4):
                                emit(i * 4 + q, q, i * 2 + (q - 2) // 2)
                        for s in range(SLOTS - 4, SLOTS + 2):
                            emit(s, s % 4, (s - 2) // 2)

                    @block.vector
                    def _(dve):
                        def clip_a(n, c):
                            dve.wait_ge(ev("up"), n + 1)
                            if later(n, 2):
                                dve.wait_ge(ev("p"), n - 1)
                            dve.tensor_scalar(a[:, c % 2, :], bank[2 + c % 2][:, 0:INNER], LIMIT * S, None, ALU.min)\
                               .then_inc(ev("a"), 1)

                        def clip_b(n, c):
                            if later(n, 2):
                                dve.wait_ge(ev("h"), n - 1)
                            dve.tensor_scalar(b[:, c % 2, :], bank[2 + c % 2][:, INNER:], LIMIT * S, -LIMIT * S,
                                              ALU.min, ALU.max).then_inc(ev("b"), 1)

                        def h_out(n, c):
                            dve.wait_ge(ev("b"), n + 1)
                            dve.wait_ge(ev("p"), n + 1)
                            if later(n, 2):
                                dve.wait_ge(ev("h_lo"), n - 1)
                            dve.scalar_tensor_tensor(h[:, c % 2, :], b[:, c % 2, :], S, p[:, c % 2, :], ALU.add,
                                                     ALU.mult).then_inc(ev("h"), 1)

                        def h_lo(n, c):
                            dve.wait_ge(ev("h_hi"), n + 1)
                            dve.tensor_tensor(hs[:, c % 2, 2:4, :], h[:, c % 2, :].rearrange("p (k n) -> p k n", k=2),
                                              hs[:, c % 2, 0:2, :], ALU.subtract).then_inc(ev("h_lo"), 1)

                        def hT_out(n, c):
                            dve.wait_ge(ev("h_turned"), n + 1)
                            if later(n, 2):
                                dve.wait_ge(ev("down"), n - 1)
                            dve.tensor_copy(hT[:, c % 2], bank16[4 + c % 2][:, 0:512].rearrange("p (q n) -> p q n", q=4))\
                               .then_inc(ev("hT"), 1)

                        def emit(s, c):
                            if there(s, 0):
                                clip_a(s, c)
                                clip_b(s, c)
                            if there(s, -1):
                                hT_out(s - 1, (c - 1) % 4)
                            if there(s, 0):
                                h_out(s, c)
                                h_lo(s, c)

                        for s in range(0, 4):
                            emit(s, s % 4)
                        with dve.Fori(1, (SLOTS - 4) // 4) as i:
                            for q in range(4):
                                emit(i * 4 + q, q)
                        for s in range(SLOTS - 4, SLOTS + 1):
                            emit(s, s % 4)

        def combine(m):
            with ExitStack() as own:
                ev = lambda name: sem(f"{name}_{m}")
                s01 = [[own.enter_context(nc.sbuf_tensor(f"sum{j}_{c}_{m}", [P, TPB, H], f32)) for j in range(2)]
                       for c in range(2)]
                back = [ev("sums_loaded0"), ev("sums_loaded1")]
                X4 = X[:, :, :].rearrange("p (b t) h -> p b t h", t=TPB)
                block = own.enter_context(nc.Block())

                @block.sync
                def _(sp):
                    with sp.Fori(0, B // 2) as i:
                        for c in range(2):
                            n = i * 2 + c
                            for j in range(2):
                                sp.dma_start(s01[c][j][:, :, :], sums[m][j][bass.ds(n * SEQ, SEQ), :]
                                             .rearrange("(t p) h -> p t h", p=P)).then_inc(back[c], 16)
                        sp.wait_ge(ev("combined"), i * 2 + 2)
                        hold(sp)
                    if m == 1:
                        for n in range(B):
                            sp.wait_ge(ev("combined"), n + 1)
                            sp.dma_start(out[n * SEQ:(n + 1) * SEQ, :].rearrange("(t p) h -> p t h", p=P),
                                         X[:, n * TPB:(n + 1) * TPB, :]).then_inc(ev("out_stored"), 16)
                        sp.wait_ge(ev("out_stored"), 16 * B)

                @block.vector
                def _(dve):
                    with dve.Fori(0, B // 2) as i:
                        for c in range(2):
                            n = i * 2 + c
                            dve.wait_ge(back[c], i * 32 + 32)
                            Xn = X4[:, bass.ds(n, 1)]
                            u, v = (s01[c][j][:, :, :].rearrange("p (o t) h -> p o t h", o=1) for j in range(2))
                            dve.tensor_tensor(u, u, v, ALU.add).then_inc(ev("summed"), 1)
                            dve.wait_ge(ev("summed"), n + 1)
                            dve.scalar_tensor_tensor(Xn, u, 0.5, Xn, ALU.mult, ALU.add).then_inc(ev("combined"), 1)

        def attention():
            with ExitStack() as own:
                def tmp(name, shape, dt=f32):
                    return own.enter_context(nc.sbuf_tensor(name, shape, dt))
                NA = 4
                alibi = tmp("alibi", [P, NA, SEQ])
                dist = tmp("dist", [P, SEQ])
                masked = tmp("masked", [P, SEQ])
                wqs = tmp("wqs", [P, HC, QG, P])
                wks = tmp("wks", [P, HC, QG, P])
                wvs = tmp("wvs", [P, HC, H])
                wos = tmp("wos", [P, HC, H])
                bqs = tmp("bqs", [P, QG])
                bks = tmp("bks", [P, QG])
                bvs = tmp("bvs", [P, H])
                bos = tmp("bos", [P, H])
                stats = tmp("stats_a", [P, TPB, 6])
                mv = tmp("mv_a", [P, TPB, 2])
                rz, shifted, root, newton = (tmp(f"{n}_a", [P, TPB]) for n in ("rz", "shifted", "root", "newton"))
                z = tmp("z_a", [P, TPB, H])
                zT = tmp("zT", [P, HC, SEQ])
                qT = tmp("qT", [P, QG, SEQ])
                kT = tmp("kT", [P, QG, SEQ])
                v = tmp("v", [P, TPB, H])
                NS = 4
                sc = tmp("sc", [P, NS, SEQ])
                mx = tmp("mx", [P, HEADS * TPB])
                nmx = tmp("nmx", [P, HEADS * TPB])
                se = tmp("se", [P, TPB, HEADS])
                re = tmp("re", [P, TPB, HEADS])
                pT = tmp("pT", [P, 2, SEQ])
                o, oT = z, zT
                attn = tmp("attn", [P, H])
                units = [(h, i) for h in range(HEADS) for i in range(TPB)]
                NU = len(units)
                s = lambda name: sem(f"att_{name}")

                with nc.Block() as block:
                    @block.sync
                    def _(sp):
                        for dst, src in ((wqs[:, :, :, :], wq), (wks[:, :, :, :], wk), (wvs[:, :, :], wv),
                                         (wos[:, :, :], wo), (bqs[:, :], bq), (bks[:, :], bk),
                                         (bvs[:, :], spread(bv)), (bos[:, :], spread(bo))):
                            sp.dma_start(dst, src).then_inc(s("loaded"), 16)
                        sp.wait_ge(s("loaded"), 16 * 8)

                    @block.gpsimd
                    def _(pool):
                        pool.iota(dist[:, :], [[1, SEQ]], P - SEQ, -1, allow_small_or_imprecise_dtypes=True)\
                            .then_inc(s("dist"), 1)
                        pool.memset(masked[:, :], 0.0).then_inc(s("dist"), 1)
                        pool.wait_ge(s("dist"), 2)
                        pool.affine_select(masked[:, :], masked[:, :], [[-1, SEQ]], ALU.is_ge, MASKED, SEQ - P, 1)\
                            .then_inc(s("dist"), 1)

                with nc.Block() as block:
                    def p_out(eng, b, n):
                        W = (units[n][1] + 1) * P
                        eng.wait_ge(s("p_turned"), b * NU + n + 1)
                        if n >= 2:
                            eng.wait_ge(s("pv"), b * NU + n - 1)
                        eng.tensor_copy(pT[:, n % 2, 0:W], bank[2 + n % 2][:, 0:W]).then_inc(s("pT"), 1)

                    @block.gpsimd
                    def _(pool):
                        with pool.Fori(0, B) as b:
                            for h in range(HEADS):
                                if h >= NA:
                                    pool.wait_ge(s("max"), b * NU + (h - NA + 1) * TPB)
                                hold(pool)
                                pool.tensor_scalar(alibi[:, h % NA, :], dist[:, :], 2.0 ** (-h / 2), None, ALU.mult)\
                                    .then_inc(s("slope"), 1)
                                pool.wait_ge(s("slope"), b * HEADS + h + 1)
                                pool.tensor_tensor(alibi[:, h % NA, :], alibi[:, h % NA, :], masked[:, :], ALU.add)\
                                    .then_inc(s("alibi"), 1)
                            pool.wait_ge(s("max"), b * NU + NU)

                    @block.vector
                    def _(dve):
                        with dve.Fori(0, B) as b:
                            for t in range(TPB):
                                dve.bn_stats(stats[:, t:t + 1, :], X[:, bass.ds(b * TPB + t, 1), :])\
                                   .then_inc(s("stats"), 1)
                            dve.wait_ge(s("stats"), b * TPB + TPB)
                            hold(dve)
                            for t in range(TPB):
                                dve.bn_aggr(mv[:, t, :], stats[:, t, :]).then_inc(s("moments"), 1)
                            dve.wait_ge(s("moments"), b * TPB + TPB)
                            rsqrt(dve, chained(dve, s("rz_steps"), b * 5), rz[:, :], mv[:, :, 1], shifted[:, :],
                                  root[:, :], newton[:, :], s("to_root"), s("rooted"), b + 1)
                            for t in range(TPB):
                                dve.tensor_scalar(z[:, t:t + 1, :], X[:, bass.ds(b * TPB + t, 1), :],
                                                  mv[:, t:t + 1, 0], rz[:, t:t + 1], ALU.subtract, ALU.mult)\
                                   .then_inc(s("z"), 1)
                            for k in range(HC):
                                dve.wait_ge(s("z_turned"), b * HC + k + 1)
                                dve.tensor_copy(zT[:, k, :], bank[k][:, :]).then_inc(s("zT"), 1)
                            for g in range(QG):
                                dve.wait_ge(s("q_product"), b * 2 * QG + g + 1)
                                dve.tensor_scalar(qT[:, g, :], bank[2 + g % 2][:, :], bqs[:, g:g + 1], 0.25, ALU.add,
                                                  ALU.mult).then_inc(s("qk"), 1)
                            for g in range(QG):
                                dve.wait_ge(s("q_product"), b * 2 * QG + QG + g + 1)
                                dve.tensor_scalar(kT[:, g, :], bank[2 + g % 2][:, :], bks[:, g:g + 1], None, ALU.add)\
                                   .then_inc(s("qk"), 1)
                            for t in range(TPB):
                                dve.wait_ge(s("v_product"), b * TPB + t + 1)
                                dve.tensor_tensor(v[:, t, :], bank[4 + t % 2][:, 0:H], bvs[:, :], ALU.add)\
                                   .then_inc(s("v"), 1)
                            for n, (h, i) in enumerate(units):
                                W = (i + 1) * P
                                dve.wait_ge(s("scores"), b * NU + n + 1)
                                if i == 0:
                                    dve.wait_ge(s("alibi"), b * HEADS + h + 1)
                                if n >= NS:
                                    dve.wait_ge(s("p_turned"), b * NU + n - NS + 1)
                                hold(dve)
                                dve.tensor_tensor_reduce(sc[:, n % NS, 0:W], bank[n % 2][:, 0:W],
                                                         alibi[:, h % NA, SEQ - W:SEQ], 1.0, MASKED, ALU.add, ALU.max,
                                                         mx[:, n:n + 1]).then_inc(s("max"), 1)
                                dve.wait_ge(s("max"), b * NU + n + 1)
                                dve.tensor_scalar(nmx[:, n:n + 1], mx[:, n:n + 1], -1.0, None, ALU.mult)\
                                   .then_inc(s("shift"), 1)
                                if n >= 2:
                                    p_out(dve, b, n - 2)
                            for n in (NU - 2, NU - 1):
                                p_out(dve, b, n)
                            dve.wait_ge(s("exp"), b * NU + NU)
                            dve.reciprocal(re[:, :, :], se[:, :, :]).then_inc(s("re"), 1)
                            dve.wait_ge(s("re"), b + 1)
                            dve.wait_ge(s("pv"), b * NU + NU)
                            for t in range(TPB):
                                dve.tensor_tensor(o[:, t, :].rearrange("p (h d) -> p h d", d=D),
                                                  bank[4 + t // 2][:, t % 2 * H:(t % 2 + 1) * H]
                                                  .rearrange("p (h d) -> p h d", d=D),
                                                  re[:, t, :].unsqueeze(2).broadcast_to([P, HEADS, D]), ALU.mult)\
                                   .then_inc(s("o"), 1)
                            for k in range(HC):
                                dve.wait_ge(s("o_turned"), b * HC + k + 1)
                                dve.tensor_copy(oT[:, k, :], bank[k][:, :]).then_inc(s("oT"), 1)
                            for t in range(TPB):
                                dve.wait_ge(s("out_product"), b * TPB + t + 1)
                                if t >= 1:
                                    dve.wait_ge(s("x"), b * TPB + t)
                                dve.tensor_tensor(attn[:, :], bank[6 + t % 2][:, 0:H], bos[:, :], ALU.add)\
                                   .then_inc(s("attn"), 1)
                                dve.wait_ge(s("attn"), b * TPB + t + 1)
                                Xt = X[:, bass.ds(b * TPB + t, 1), :]
                                dve.tensor_tensor(Xt, Xt, attn[:, :].rearrange("p (o h) -> p o h", o=1), ALU.add)\
                                   .then_inc(s("x"), 1)

                    @block.scalar
                    def _(act):
                        with act.Fori(0, B) as b:
                            act.wait_ge(s("to_root"), b + 1)
                            act.activation(root[:, :], shifted[:, :], ACT.Sqrt).then_inc(s("rooted"), 1)
                            for n, (h, i) in enumerate(units):
                                W = (i + 1) * P
                                act.wait_ge(s("shift"), b * NU + n + 1)
                                act.activation(sc[:, n % NS, 0:W], sc[:, n % NS, 0:W], ACT.Exp, bias=nmx[:, n:n + 1],
                                               accum_out=se[:, i, h:h + 1]).then_inc(s("exp"), 1)

                    @block.tensor
                    def _(pe):
                        def turn_p(b, n):
                            pe.wait_ge(s("exp"), b * NU + n + 1)
                            if n >= 2:
                                pe.wait_ge(s("pT"), b * NU + n - 1)
                            for j in range(units[n][1] + 1):
                                mm = pe.transpose(bank[2 + n % 2][:, j * P:(j + 1) * P],
                                                  sc[:, n % NS, j * P:(j + 1) * P], ident[:, :])
                            mm.then_inc(s("p_turned"), 1)

                        def weigh(b, n):
                            h, i = units[n]
                            pe.wait_ge(s("pT"), b * NU + n + 1)
                            for j in range(i + 1):
                                mm = pe.matmul(bank[4 + i // 2][:, i % 2 * H + h * D:i % 2 * H + (h + 1) * D],
                                               pT[:, n % 2, j * P:(j + 1) * P], v[:, j, h * D:(h + 1) * D],
                                               start=(j == 0), stop=(j == i))
                            mm.then_inc(s("pv"), 1)

                        with pe.Fori(0, B) as b:
                            for k in range(HC):
                                for t in range(TPB):
                                    if k == 0:
                                        pe.wait_ge(s("z"), b * TPB + t + 1)
                                    mm = pe.transpose(bank[k][:, t * P:(t + 1) * P], z[:, t, k * P:(k + 1) * P],
                                                      ident[:, :])
                                mm.then_inc(s("z_turned"), 1)
                            pe.wait_ge(s("zT"), b * HC + HC)
                            for c, w in enumerate((wqs, wks)):
                                for g in range(QG):
                                    n = c * QG + g
                                    if n >= 2:
                                        pe.wait_ge(s("qk"), b * 2 * QG + n - 1)
                                    for k in range(HC):
                                        mm = pe.matmul(bank[2 + g % 2][:, :], w[:, k, g, :], zT[:, k, :],
                                                       start=(k == 0), stop=(k == HC - 1))
                                    mm.then_inc(s("q_product"), 1)
                            for t in range(TPB):
                                if t >= 2:
                                    pe.wait_ge(s("v"), b * TPB + t - 1)
                                for k in range(HC):
                                    mm = pe.matmul(bank[4 + t % 2][:, 0:H], zT[:, k, t * P:(t + 1) * P], wvs[:, k, :],
                                                   start=(k == 0), stop=(k == HC - 1))
                                mm.then_inc(s("v_product"), 1)
                            pe.wait_ge(s("qk"), b * 2 * QG + 2 * QG)
                            pe.wait_ge(s("v"), b * TPB + TPB)
                            for n, (h, i) in enumerate(units):
                                g, r = h // 4, h % 4 * 32
                                if n >= 2:
                                    pe.wait_ge(s("max"), b * NU + n - 1)
                                pe.matmul(bank[n % 2][:, 0:(i + 1) * P], qT[r:r + D, g, i * P:(i + 1) * P],
                                          kT[r:r + D, g, 0:(i + 1) * P], start=True, stop=True,
                                          tile_position=(r, 0)).then_inc(s("scores"), 1)
                                if n >= 2:
                                    turn_p(b, n - 2)
                                if n >= 3:
                                    weigh(b, n - 3)
                            for n in (NU - 2, NU - 1):
                                turn_p(b, n)
                                weigh(b, n - 1)
                            weigh(b, NU - 1)
                            for k in range(HC):
                                for t in range(TPB):
                                    if k == 0:
                                        pe.wait_ge(s("o"), b * TPB + t + 1)
                                    mm = pe.transpose(bank[k][:, t * P:(t + 1) * P], o[:, t, k * P:(k + 1) * P],
                                                      ident[:, :])
                                mm.then_inc(s("o_turned"), 1)
                            pe.wait_ge(s("oT"), b * HC + HC)
                            for t in range(TPB):
                                if t >= 2:
                                    pe.wait_ge(s("attn"), b * TPB + t - 1)
                                for k in range(HC):
                                    mm = pe.matmul(bank[6 + t % 2][:, 0:H], oT[:, k, t * P:(t + 1) * P], wos[:, k, :],
                                                   start=(k == 0), stop=(k == HC - 1))
                                mm.then_inc(s("out_product"), 1)

        def moe(m):
            with ExitStack() as own:
                tabs = [own.enter_context(nc.sbuf_tensor(f"{n}{m}", [P, SLOTS], dt))
                        for n, dt in (("gather_at", u32), ("add_at", u32), ("gate_at", f32), ("expert_at", i32))]
                route(m, *tabs)
                experts(m, *tabs)
            combine(m)

        setup()
        moe(0)
        end_phase()
        attention()
        end_phase()
        moe(1)
        end_phase()


def kernel(L0_attn_x, L0_attn_Wqkv, L0_attn_bqkv, L0_attn_Wo, L0_attn_bo, L0_ffn_norm_w, L0_ffn_gate_w,
           L0_ffn_gate_b, L0_ffn_w1, L0_ffn_b1, L0_ffn_w2, L0_ffn_b2):
    import numpy as np
    import concourse.bacc as bacc
    from concourse.bass_utils import run_bass_kernel_spmd

    def chunks(w):
        return w.reshape(-1, P, w.shape[-1]).transpose(1, 0, 2)

    def heads_at_32(w):
        wide = np.zeros((w.shape[0], HEADS, 32), w.dtype)
        wide[:, :, 0:D] = w.reshape(w.shape[0], HEADS, D)
        return wide.reshape(w.shape[0], HEADS * 32)

    Wqkv, bqkv = np.asarray(L0_attn_Wqkv), np.asarray(L0_attn_bqkv)
    w1 = np.asarray(L0_ffn_w1).transpose(0, 2, 1)
    w1 = w1.reshape(E, H, INNER, 2).transpose(0, 1, 3, 2)
    w1 = w1.reshape(E, HC, P, 2 * INNER).transpose(0, 2, 1, 3)
    w2 = np.asarray(L0_ffn_w2).transpose(0, 2, 1).reshape(E, 2, P, H).transpose(0, 2, 1, 3)
    split = [Wqkv[:, i * H:(i + 1) * H] for i in range(3)]
    arrays = {
        "x": np.asarray(L0_attn_x).reshape(T, H),
        "wq": chunks(heads_at_32(split[0])).reshape(P, HC, QG, P),
        "wk": chunks(heads_at_32(split[1])).reshape(P, HC, QG, P),
        "wv": chunks(split[2]),
        "bq": heads_at_32(bqkv[None, 0:H]).reshape(QG, P).T,
        "bk": heads_at_32(bqkv[None, H:2 * H]).reshape(QG, P).T,
        "bv": bqkv[2 * H:],
        "wo": chunks(np.asarray(L0_attn_Wo)),
        "bo": np.asarray(L0_attn_bo),
        "norm_w": np.asarray(L0_ffn_norm_w),
        "gate_w": chunks(np.asarray(L0_ffn_gate_w).T),
        "gate_b": np.asarray(L0_ffn_gate_b),
        "w1": w1.reshape(E, P, HC * 2 * INNER),
        "b1": np.asarray(L0_ffn_b1).reshape(E, INNER, 2).transpose(0, 2, 1).reshape(E, 2 * INNER),
        "w2": w2.reshape(E, P, 2 * H),
        "b2": np.asarray(L0_ffn_b2),
    }
    nc = bacc.Bacc("TRN2", target_bir_lowering=False, num_devices=1)
    feeds, args = {}, []
    for name, a in arrays.items():
        a = np.ascontiguousarray(a)
        feeds[f"in_{name}"] = a
        args.append(nc.dram_tensor(f"in_{name}", a.shape, mybir.dt.from_np(a.dtype), kind="ExternalInput").ap())
    out = nc.dram_tensor("out", (T, H), f32, kind="ExternalOutput").ap()
    build(nc, *args, out)
    result = run_bass_kernel_spmd(nc, [feeds], core_ids=[0])
    return result.results[0]["out"].reshape(B, SEQ, H)
```

```python
import concourse.bass as bass
from concourse import mybir
from contextlib import ExitStack

f32 = mybir.dt.float32
f16 = mybir.dt.float16
bf16 = mybir.dt.bfloat16
u32 = mybir.dt.uint32
i32 = mybir.dt.int32
ALU = mybir.AluOpType
ACT = mybir.ActivationFunctionType
AX = mybir.AxisListType

P = 128
B, SEQ, H = 4, 512, 256
T = B * SEQ
NT = T // P
TPB = SEQ // P
HC = H // P
E, K, INNER = 16, 4, 256
SLOTS = 80
HEADS, D = 16, 16
HG = P // 32
QG = HEADS // HG
EPS = 1e-5
LIMIT = 7.0
TS = 2.0 ** 4
WS = 2.0 ** 6
S = TS * WS
MASKED = -1e30


def build(nc, x, wqkv, bias_qk, bv, wo, bo, query_rows, key_rows, norm_w, gate_w, gate_b, w1, b1, w2, b2, out):
    ctx = ExitStack()
    known = {}
    holds = nc.alloc_semaphore("holds")

    def sem(name):
        if name not in known:
            known[name] = nc.alloc_semaphore(name)
        return known[name]

    def end_phase():
        nc.clear_and_free_semaphores(list(known.values()))
        known.clear()
        nc.all_engine_barrier()

    def keep(name, shape, dt=f32):
        return ctx.enter_context(nc.sbuf_tensor(name, shape, dt))

    def spread(vector, n=P):
        return vector.rearrange("(a n) -> a n", a=1).broadcast_to([n, vector.shape[0]])

    def chained(eng, s, start=0):
        count = [start]

        def step(instruction):
            count[0] += 1
            instruction.then_inc(s, 1)
            eng.wait_ge(s, count[0])
        return step

    def hold(eng):
        eng.sem_inc(holds, 1)

    def rounds(eng, count, emit):
        emit(0)
        with eng.Fori(1, count) as i:
            emit(i)

    def later(n, first):
        return not isinstance(n, int) or n >= first

    def rsqrt(dve, step, out_, var, shifted, root, newton, to_root, rooted, value):
        dve.tensor_scalar(shifted, var, EPS, None, ALU.add).then_inc(to_root, 1)
        dve.wait_ge(rooted, value)
        step(dve.reciprocal(out_, root))
        step(dve.tensor_tensor(newton, out_, out_, ALU.mult))
        step(dve.tensor_tensor(newton, newton, shifted, ALU.mult))
        step(dve.tensor_scalar(newton, newton, -0.5, 1.5, ALU.mult, ALU.add))
        step(dve.tensor_tensor(out_, out_, newton, ALU.mult))

    with ctx:
        t_rows = [nc.dram_tensor(f"t_rows{m}", (T, 2 * H), f16, kind="Internal").ap() for m in range(2)]
        sums = [[nc.dram_tensor(f"sums{m}_{j}", (T + P, H), f32, kind="Internal").ap() for j in range(2)]
                for m in range(2)]
        bias_dram = nc.dram_tensor("bias_split", (2, E, 2 * INNER), f16, kind="Internal").ap()

        X = keep("X", [P, NT, H])
        w1s = keep("w1s", [P, E, HC, 2, 2 * INNER], f16)
        w2s = keep("w2s", [P, E, 2, 2, H], f16)
        ones16 = keep("ones16", [P, P], f16)
        ident = keep("ident", [P, P])
        ident16 = keep("ident16", [P, P], f16)
        before = keep("before", [P, P], f16)
        normw = keep("normw", [P, H])
        gatew = keep("gatew", [P, HC, E])
        gateb = keep("gateb", [P, E])
        b2r = keep("b2r", [E, H])
        iota_e = keep("iota_e", [P, E])
        iota_t = keep("iota_t", [P, SLOTS])
        iota_t16 = keep("iota_t16", [P, SLOTS], f16)
        iota_p16 = keep("iota_p16", [P, P], f16)
        tok = keep("tok", [P, NT])
        idle = keep("idle", [P, 1])
        bank = [ctx.enter_context(nc.psum_tensor(f"bank{i}", [P, 512], f32)) for i in range(8)]
        bank16 = [b[:, :].bitcast(f16) for b in bank]

        def setup():
            with ExitStack() as own:
                N1, N2 = HC * 2 * INNER, 2 * H
                NW = 8
                stage = [own.enter_context(nc.sbuf_tensor(f"stage{j}", [P, N1 + N2], f32)) for j in range(NW)]
                b1_raw = own.enter_context(nc.sbuf_tensor("b1_raw", [E, 2 * INNER], f32))
                b1_hi = own.enter_context(nc.sbuf_tensor("b1_hi", [E, 2 * INNER], f16))
                b1_lo = own.enter_context(nc.sbuf_tensor("b1_lo", [E, 2 * INNER], f16))
                loaded = [sem(f"weights_loaded{j}") for j in range(NW)]
                view1 = lambda j: stage[j][:, 0:N1].rearrange("p (e k n) -> p e k n", e=1, k=HC)
                view2 = lambda j: stage[j][:, N1:].rearrange("p (e k n) -> p e k n", e=1, k=2)
                block = own.enter_context(nc.Block())

                @block.sync
                def _(sp):
                    sp.dma_start(b1_raw[:, :], b1).then_inc(sem("b1_loaded"), 16)
                    for dst, src in ((normw[:, :], spread(norm_w)), (gateb[:, :], spread(gate_b)),
                                     (gatew[:, :, :], gate_w), (b2r[:, :], b2),
                                     (X[:, :, :], x.rearrange("(t p) h -> p t h", p=P))):
                        sp.dma_start(dst, src).then_inc(sem("inputs_loaded"), 16)
                    def emit(i):
                        for j in range(NW):
                            if later(i, 1):
                                sp.wait_ge(sem("lo_split"), (i - 1) * NW + j + 1)
                                hold(sp)
                            sp.dma_start(stage[j][:, 0:N1], w1[bass.ds(i * NW + j, 1)].rearrange("e p n -> p (e n)"))\
                              .then_inc(loaded[j], 16)
                            sp.dma_start(stage[j][:, N1:], w2[bass.ds(i * NW + j, 1)].rearrange("e p n -> p (e n)"))\
                              .then_inc(loaded[j], 16)
                    rounds(sp, E // NW, emit)
                    sp.wait_ge(sem("b1_split"), 2)
                    sp.dma_start(bias_dram[0], b1_hi[:, :]).then_inc(sem("b1_stored"), 16)
                    sp.dma_start(bias_dram[1], b1_lo[:, :]).then_inc(sem("b1_stored"), 16)
                    sp.wait_ge(sem("b1_stored"), 32)
                    sp.wait_ge(sem("inputs_loaded"), 16 * 5)

                @block.scalar
                def _(act):
                    act.wait_ge(sem("b1_loaded"), 16)
                    act.activation(b1_hi[:, :], b1_raw[:, :], ACT.Copy, scale=S).then_inc(sem("b1_split"), 1)
                    with act.Fori(0, E // NW) as i:
                        for j in range(NW):
                            e = bass.ds(i * NW + j, 1)
                            act.wait_ge(loaded[j], i * 32 + 32)
                            act.activation(w1s[:, e, :, 0, :], view1(j), ACT.Copy, scale=WS)
                            act.activation(w2s[:, e, :, 0, :], view2(j), ACT.Copy, scale=WS)\
                               .then_inc(sem("hi_split"), 1)

                @block.vector
                def _(dve):
                    dve.wait_ge(sem("b1_split"), 1)
                    dve.scalar_tensor_tensor(b1_lo[:, :], b1_raw[:, :], S, b1_hi[:, :], ALU.mult, ALU.subtract)\
                       .then_inc(sem("b1_split"), 1)
                    with dve.Fori(0, E // NW) as i:
                        for j in range(NW):
                            e = bass.ds(i * NW + j, 1)
                            dve.wait_ge(sem("hi_split"), i * NW + j + 1)
                            dve.scalar_tensor_tensor(w1s[:, e, :, 1, :], view1(j), WS, w1s[:, e, :, 0, :],
                                                     ALU.mult, ALU.subtract)
                            dve.scalar_tensor_tensor(w2s[:, e, :, 1, :], view2(j), WS, w2s[:, e, :, 0, :],
                                                     ALU.mult, ALU.subtract).then_inc(sem("lo_split"), 1)

                @block.gpsimd
                def _(pool):
                    made = sem("constants")
                    pool.memset(ones16[:, :], 1.0).then_inc(made, 1)
                    pool.memset(ident[:, :], 0.0).then_inc(made, 1)
                    pool.memset(ident16[:, :], 0.0).then_inc(made, 1)
                    for dst, step, base, per_partition in ((iota_e, 1, 0, 0), (iota_t, 1, 0, 0), (iota_p16, 1, 0, 0), (iota_t16, 1, 0, 0),
                                                           (tok, P, 1, 1), (idle, 1, T + 1, 1)):
                        pool.iota(dst[:, :], [[step, dst.shape[1]]], base, per_partition,
                                  allow_small_or_imprecise_dtypes=True).then_inc(made, 1)
                    pool.wait_ge(made, 9)
                    for square in (ident, ident16):
                        pool.affine_select(square[:, :], square[:, :], [[-1, P]], ALU.not_equal, 1.0, 0, 1)\
                            .then_inc(made, 1)
                    pool.affine_select(before[:, :], ones16[:, :], [[1, P]], ALU.is_gt, 0.0, 0, -1)\
                        .then_inc(made, 1)

        def route(m, b1s, gather_at, add_at, gate_at, expert_at):
            with ExitStack() as own:
                def tmp(name, shape, dt=f32):
                    return own.enter_context(nc.sbuf_tensor(f"{name}_r{m}", shape, dt))
                ev = lambda name: sem(f"{name}_{m}")
                NB = 2
                stats = tmp("stats", [P, NT, 6])
                mv = tmp("mv", [P, NT, 2])
                rz = tmp("rz", [P, NT])
                rt = tmp("rt", [P, NT])
                shifted = tmp("shifted", [P, NT])
                root = tmp("root", [P, NT])
                newton = tmp("newton", [P, NT])
                meansq = tmp("meansq", [P, NT])
                z = tmp("z", [P, NB, H])
                t = tmp("t", [P, NB, H])
                row = tmp("row", [P, NB, 2 * H], f16)
                tT = tmp("tT", [P, NB, HC, P])
                logits = tmp("logits", [P, NT, E])
                row_stored = [ev(f"row_stored{j}") for j in range(NB)]

                with nc.Block() as block:
                    @block.gpsimd
                    def _(pool):
                        pool.memset(b1s[:, :, :], 0.0).then_inc(ev("b1_zeroed"), 1)

                    @block.vector
                    def _(dve):
                        for i in range(NT):
                            dve.bn_stats(stats[:, i, :], X[:, i, :]).then_inc(ev("stats"), 1)
                        for i in range(NT):
                            dve.wait_ge(ev("stats"), i + 1)
                            dve.bn_aggr(mv[:, i, :], stats[:, i, :]).then_inc(ev("moments"), 1)
                        dve.wait_ge(ev("moments"), NT)
                        step = chained(dve, ev("scales"))
                        rsqrt(dve, step, rz[:, :], mv[:, :, 1], shifted[:, :], root[:, :], newton[:, :],
                              ev("to_root"), ev("rooted"), 1)
                        step(dve.tensor_tensor(rt[:, :], rz[:, :], rz[:, :], ALU.mult))
                        step(dve.tensor_tensor(meansq[:, :], rt[:, :], mv[:, :, 1], ALU.mult))
                        rsqrt(dve, step, rt[:, :], meansq[:, :], shifted[:, :], root[:, :], newton[:, :],
                              ev("to_root"), ev("rooted"), 2)
                        step(dve.tensor_scalar(rt[:, :], rt[:, :], TS, None, ALU.mult))
                        def logits_out(n, j):
                            dve.wait_ge(ev("gate_product"), n + 1)
                            dve.scalar_tensor_tensor(
                                logits[:, bass.ds(n, 1), :], bank[2 + j][:, 0:E].rearrange("p (o e) -> p o e", o=1),
                                1.0 / TS, gateb[:, :].rearrange("p (o e) -> p o e", o=1), ALU.mult, ALU.add)\
                               .then_inc(ev("logits"), 1)

                        def emit(i):
                            for j in range(NB):
                                n = i * NB + j
                                one = bass.ds(n, 1)
                                dve.tensor_scalar(z[:, j:j + 1, :], X[:, one, :], mv[:, one, 0], rz[:, one],
                                                  ALU.subtract, ALU.mult).then_inc(ev("z"), 1)
                                dve.wait_ge(ev("z"), n + 1)
                                dve.scalar_tensor_tensor(t[:, j, :], z[:, j, :], rt[:, one], normw[:, :],
                                                         ALU.mult, ALU.mult).then_inc(ev("t"), 1)
                                if later(n, 1):
                                    logits_out(n - 1, (j - 1) % NB)
                                dve.wait_ge(ev("row_hi"), n + 1)
                                dve.tensor_tensor(row[:, j, H:], t[:, j, :], row[:, j, 0:H], ALU.subtract)\
                                   .then_inc(ev("row_lo"), 1)
                        rounds(dve, NT // NB, emit)
                        logits_out(NT - 1, (NT - 1) % NB)

                    @block.scalar
                    def _(act):
                        for n in range(2):
                            act.wait_ge(ev("to_root"), n + 1)
                            act.activation(root[:, :], shifted[:, :], ACT.Sqrt).then_inc(ev("rooted"), 1)
                        def emit(i):
                            for j in range(NB):
                                n = i * NB + j
                                if later(i, 1):
                                    act.wait_ge(row_stored[j], i * 16)
                                act.wait_ge(ev("t"), n + 1)
                                act.activation(row[:, j, 0:H], t[:, j, :], ACT.Copy).then_inc(ev("row_hi"), 1)
                                act.wait_ge(ev("t_turned"), n + 1)
                                act.activation(tT[:, j], bank[j][:, 0:H].rearrange("p (k n) -> p k n", k=HC),
                                               ACT.Copy).then_inc(ev("tT"), 1)
                        rounds(act, NT // NB, emit)

                    @block.tensor
                    def _(pe):
                        with pe.Fori(0, NT // NB) as i:
                            for j in range(NB):
                                n = i * NB + j
                                pe.wait_ge(ev("t"), n + 1)
                                for k in range(HC):
                                    mm = pe.transpose(bank[j][:, k * P:(k + 1) * P], t[:, j, k * P:(k + 1) * P],
                                                      ident[:, :])
                                mm.then_inc(ev("t_turned"), 1)
                                pe.wait_ge(ev("tT"), n + 1)
                                for k in range(HC):
                                    mm = pe.matmul(bank[2 + j][:, 0:E], tT[:, j, k, :], gatew[:, k, :],
                                                   start=(k == 0), stop=(k == HC - 1))
                                mm.then_inc(ev("gate_product"), 1)

                    @block.sync
                    def _(sp):
                        sp.wait_ge(ev("b1_zeroed"), 1)
                        sp.dma_start(b1s[0:2, :, :], bias_dram).then_inc(ev("b1s_loaded"), 16)
                        with sp.Fori(0, NT // NB) as i:
                            for j in range(NB):
                                n = i * NB + j
                                sp.wait_ge(ev("row_lo"), n + 1)
                                sp.dma_start(t_rows[m][bass.ds(n * P, P), :], row[:, j, :]).then_inc(row_stored[j], 16)
                        for j in range(NB):
                            sp.wait_ge(row_stored[j], 16 * NT // NB)
                        sp.wait_ge(ev("b1s_loaded"), 16)

                top = tmp("top", [P, NT, 8])
                topi = tmp("topi", [P, NT, 8], u32)
                topf = tmp("topf", [P, NT, K])
                ex = tmp("ex", [P, NT, K])
                total = tmp("total", [P, NT])
                gate = tmp("gate", [P, NT, K])
                chosen = tmp("chosen", [P, NT, K, E])
                work = tmp("work", [P, NT, K, E])
                mask16 = tmp("mask16", [P, NT, E], f16)
                gates = tmp("gates", [P, NT, E])
                count = tmp("count", [P, E], i32)
                tiles = tmp("tiles", [P, E])
                end = tmp("end", [P, E])
                ones_e = tmp("ones_e", [P, E])
                pos = tmp("pos", [P, NT, E])
                slot = tmp("slot", [P, NT, K], i32)
                slot_low = tmp("slot_low", [P, NT, K], i32)
                slot_f = tmp("slot_f", [P, NT, K])
                slot_row = tmp("slot_row", [P, NT, K], f16)
                slot_tile = tmp("slot_tile", [P, NT, K], f16)
                gate_hi = tmp("gate_hi", [P, NT, K], f16)
                gate_hi32 = tmp("gate_hi32", [P, NT, K])
                gate_lo = tmp("gate_lo", [P, NT, K], f16)
                passed = tmp("passed", [P, SLOTS, E])
                expert_f = tmp("expert_f", [P, SLOTS])
                hot_row = tmp("hot_row", [P, 2, K, P], f16)
                hot_tile = tmp("hot_tile", [P, 2, K, SLOTS], f16)
                hot_value = tmp("hot_value", [P, 2, K, 3, SLOTS], f16)
                zeros = tmp("zeros", [P, 3 * SLOTS], f16)
                gT = tmp("gT", [E, T])
                idles = tmp("idles", [P, SLOTS])
                table = tmp("table", [P, 3, SLOTS])
                first = tmp("first", [P, 2, H])
                first_stored = [ev("first_stored0"), ev("first_stored1")]
                zero_sum = tmp("zero_sum", [P, H])

                with nc.Block() as block:
                    @block.vector
                    def _(dve):
                        dve.memset(zeros[:, :], 0.0).then_inc(ev("zeroed"), 1)
                        dve.memset(zero_sum[:, :], 0.0).then_inc(ev("zeroed"), 1)
                        dve.memset(ones_e[:, :], 1.0).then_inc(ev("zeroed"), 1)
                        dve.wait_ge(ev("zeroed"), 3)
                        for i in range(NT):
                            dve.max(top[:, i, :], logits[:, i, :]).then_inc(ev("top"), 1)
                        for i in range(NT):
                            dve.wait_ge(ev("top"), i + 1)
                            dve.max_index(topi[:, i, :], top[:, i, :], logits[:, i, :]).then_inc(ev("topi"), 1)
                        dve.tensor_tensor(ex[:, :, :], top[:, :, 0:K], top[:, :, 0:1].broadcast_to([P, NT, K]),
                                          ALU.subtract).then_inc(ev("shifted"), 1)
                        dve.wait_ge(ev("topi"), NT)
                        step = chained(dve, ev("route_steps"))
                        step(dve.tensor_copy(topf[:, :, :], topi[:, :, 0:K]))
                        step(dve.tensor_tensor(chosen[:, :, :, :],
                                               topf[:, :, :].unsqueeze(3).broadcast_to([P, NT, K, E]),
                                               iota_e[:, :].unsqueeze(1).unsqueeze(1).broadcast_to([P, NT, K, E]),
                                               ALU.is_equal))
                        with nc.allow_low_precision("zeros and ones"):
                            dve.tensor_reduce(mask16[:, :, :], chosen[:, :, :, :].rearrange("p t k e -> p t e k"),
                                              AX.X, ALU.add).then_inc(ev("mask"), 1)
                        dve.wait_ge(ev("exps"), 1)
                        step(dve.tensor_reduce(total[:, :], ex[:, :, :], AX.X, ALU.add))
                        step(dve.reciprocal(total[:, :], total[:, :]))
                        step(dve.tensor_tensor(gate[:, :, :], ex[:, :, :],
                                               total[:, :].unsqueeze(2).broadcast_to([P, NT, K]), ALU.mult))
                        step(dve.tensor_copy(gate_hi[:, :, :], gate[:, :, :]))
                        step(dve.tensor_copy(gate_hi32[:, :, :], gate_hi[:, :, :]))
                        step(dve.tensor_tensor(gate_lo[:, :, :], gate[:, :, :], gate_hi[:, :, :], ALU.subtract))
                        step(dve.tensor_tensor(work[:, :, :, :], chosen[:, :, :, :],
                                               gate[:, :, :].unsqueeze(3).broadcast_to([P, NT, K, E]), ALU.mult))
                        dve.tensor_reduce(gates[:, :, :], work[:, :, :, :].rearrange("p t k e -> p t e k"),
                                          AX.X, ALU.add).then_inc(ev("gates"), 1)
                        dve.wait_ge(ev("gates"), 1)
                        dve.wait_ge(ev("ranks"), 1)
                        step(dve.tensor_scalar(count[:, :], bank[1][:, 0:E], P - 1.0, None, ALU.add))
                        step(dve.tensor_scalar(count[:, :], count[:, :], 7, None, ALU.arith_shift_right))
                        step(dve.tensor_copy(tiles[:, :], count[:, :]))
                        step(dve.tensor_tensor_scan(end[:, :], ones_e[:, :], tiles[:, :], 0.0, ALU.mult, ALU.add))
                        step(dve.tensor_tensor(tiles[:, :], end[:, :], tiles[:, :], ALU.subtract))
                        step(dve.tensor_scalar(tiles[:, :], tiles[:, :], float(P), None, ALU.mult))
                        step(dve.tensor_tensor(pos[:, :, :], bank[0][:, 0:NT * E].rearrange("p (t e) -> p t e", e=E),
                                               tiles[:, :].unsqueeze(1).broadcast_to([P, NT, E]), ALU.add))
                        step(dve.tensor_tensor(work[:, :, :, :], chosen[:, :, :, :],
                                               pos[:, :, :].unsqueeze(2).broadcast_to([P, NT, K, E]), ALU.mult))
                        step(dve.tensor_reduce(slot_f[:, :, :], work[:, :, :, :], AX.X, ALU.add))
                        step(dve.tensor_copy(slot[:, :, :], slot_f[:, :, :]))
                        step(dve.tensor_scalar(slot_low[:, :, :], slot[:, :, :], P - 1, None, ALU.bitwise_and))
                        step(dve.tensor_scalar(slot[:, :, :], slot[:, :, :], 7, None, ALU.arith_shift_right))
                        step(dve.tensor_copy(slot_row[:, :, :], slot_low[:, :, :]))
                        step(dve.tensor_copy(slot_tile[:, :, :], slot[:, :, :]))
                        def place(i):
                            for j in range(2):
                                n = i * 2 + j
                                one = bass.ds(n, 1)
                                if later(i, 1):
                                    dve.wait_ge(ev("placed"), n - 1)
                                hot = lambda tile, j=j: tile[:, j].rearrange("p (o k) s -> p o k s", o=1)
                                dve.tensor_tensor(hot(hot_tile),
                                                  slot_tile[:, one, :].unsqueeze(3).broadcast_to([P, 1, K, SLOTS]),
                                                  iota_t16[:, :].unsqueeze(1).unsqueeze(1)
                                                  .broadcast_to([P, 1, K, SLOTS]), ALU.is_equal)\
                                   .then_inc(ev("hot_tile"), 1)
                                dve.tensor_tensor(hot(hot_row),
                                                  slot_row[:, one, :].unsqueeze(3).broadcast_to([P, 1, K, P]),
                                                  iota_p16[:, :].unsqueeze(1).unsqueeze(1)
                                                  .broadcast_to([P, 1, K, P]), ALU.is_equal)
                                dve.wait_ge(ev("hot_tile"), n + 1)
                                dve.tensor_scalar(hot_value[:, j, :, 0, :], hot_tile[:, j], tok[:, one], None,
                                                  ALU.mult).then_inc(ev("hot_token"), 1)
                        rounds(dve, NT // 2, place)
                        step(dve.tensor_tensor(passed[:, :, :], end[:, :].unsqueeze(1).broadcast_to([P, SLOTS, E]),
                                               iota_t[:, :].unsqueeze(2).broadcast_to([P, SLOTS, E]), ALU.is_le))
                        step(dve.tensor_reduce(expert_f[:, :], passed[:, :, :], AX.X, ALU.add))
                        step(dve.tensor_scalar(expert_at[:, :], expert_f[:, :], E - 1.0, None, ALU.min))
                        dve.wait_ge(ev("placed_all"), 1)
                        step(dve.tensor_copy(table[:, :, :], bank[2][:, 0:3 * SLOTS].rearrange("p (a s) -> p a s", a=3)))
                        step(dve.tensor_tensor(table[:, 1, :], table[:, 1, :], table[:, 2, :], ALU.add))
                        step(dve.tensor_scalar(gather_at[:, :], table[:, 0, :], -1.0, 0.0, ALU.add, ALU.max))
                        step(dve.tensor_scalar(idles[:, :], table[:, 0, :], 0.0, idle[:, 0:1], ALU.is_equal, ALU.mult))
                        step(dve.scalar_tensor_tensor(add_at[:, :], table[:, 0, :], -1.0, idles[:, :],
                                                      ALU.add, ALU.add))
                        step(dve.tensor_scalar(gate_at[:, :], table[:, 1, :], 1.0 / (S * WS), None, ALU.mult))
                        def start_sums(i):
                            for j in range(2):
                                n = i * 2 + j
                                one = bass.ds(n, 1)
                                if later(i, 1):
                                    dve.wait_ge(first_stored[j], i * 16)
                                dve.tensor_scalar(z[:, j:j + 1, :], X[:, one, :], mv[:, one, 0], rz[:, one],
                                                  ALU.subtract, ALU.mult).then_inc(ev("z_again"), 1)
                                dve.wait_ge(ev("z_again"), n + 1)
                                dve.wait_ge(ev("bias_product"), n + 1)
                                dve.tensor_tensor(first[:, j, :], z[:, j, :], bank[5 + j][:, 0:H], ALU.add)\
                                   .then_inc(ev("first"), 1)
                        rounds(dve, NT // 2, start_sums)

                    @block.gpsimd
                    def _(pool):
                        def emit(i):
                            for j in range(2):
                                n = i * 2 + j
                                if later(i, 1):
                                    pool.wait_ge(ev("placed"), n - 1)
                                pool.wait_ge(ev("hot_tile"), n + 1)
                                hold(pool)
                                pool.tensor_tensor(hot_value[:, j, :, 2, :].rearrange("p (o k) s -> p o k s", o=1),
                                                   hot_tile[:, j].rearrange("p (o k) s -> p o k s", o=1),
                                                   gate_lo[:, bass.ds(n, 1), :].unsqueeze(3)
                                                   .broadcast_to([P, 1, K, SLOTS]), ALU.mult)\
                                    .then_inc(ev("hot_lo"), 1)
                        rounds(pool, NT // 2, emit)

                    @block.scalar
                    def _(act):
                        act.wait_ge(ev("shifted"), 1)
                        act.activation(ex[:, :, :], ex[:, :, :], ACT.Exp).then_inc(ev("exps"), 1)
                        for g in range(NT // 4):
                            act.wait_ge(ev("gates_turned"), g + 1)
                            act.activation(gT[:, g * 512:(g + 1) * 512], bank[3 + g % 2][0:E, :], ACT.Copy)\
                               .then_inc(ev("gT"), 1)
                        def emit(i):
                            for j in range(2):
                                n = i * 2 + j
                                if later(i, 1):
                                    act.wait_ge(ev("placed"), n - 1)
                                act.wait_ge(ev("hot_tile"), n + 1)
                                for k in range(K):
                                    mul = act.activation(hot_value[:, j, k, 1:2, :], hot_tile[:, j, k:k + 1, :], ACT.Copy,
                                                         scale=gate_hi32[:, bass.ds(n, 1), k])
                                mul.then_inc(ev("hot_hi"), 1)
                        rounds(act, NT // 2, emit)

                    @block.tensor
                    def _(pe):
                        pe.wait_ge(ev("mask"), 1)
                        flat = mask16[:, :, :].rearrange("p t e -> p (t e)")
                        for i in range(NT - 1):
                            later = NT - 1 - i
                            pe.matmul(bank[0][:, (i + 1) * E:NT * E].rearrange("p (t e) -> p t e", e=E), ones16[:, :],
                                      mask16[:, i:i + 1, :].broadcast_to([P, later, E]), start=(i == 0),
                                      stop=False, skip_group_check=True)
                        pe.matmul(bank[0][:, 0:NT * E], before[:, :], flat, start=False, stop=True,
                                  skip_group_check=True)
                        for i in range(NT):
                            mm = pe.matmul(bank[1][:, 0:E], ones16[:, :], mask16[:, i, :], start=(i == 0),
                                           stop=(i == NT - 1))
                        mm.then_inc(ev("ranks"), 1)
                        pe.wait_ge(ev("gates"), 1)
                        for g in range(NT // 4):
                            if g >= 2:
                                pe.wait_ge(ev("gT"), g - 1)
                            for c in range(4):
                                mm = pe.transpose(bank[3 + g % 2][0:E, c * P:(c + 1) * P], gates[:, 4 * g + c, :],
                                                  ident[:, :])
                            mm.then_inc(ev("gates_turned"), 1)
                        pe.wait_ge(ev("zeroed"), 3)
                        o = bank[2][:, 0:3 * SLOTS]
                        pe.matmul(o, zeros[:, 0:P], zeros[:, :], start=True, stop=False, skip_group_check=True)
                        with pe.Fori(0, NT // 2) as i:
                            for j in range(2):
                                for part in ("hot_token", "hot_hi", "hot_lo"):
                                    pe.wait_ge(ev(part), i * 2 + j + 1)
                                for k in range(K):
                                    mm = pe.matmul(o, hot_row[:, j, k, :],
                                                   hot_value[:, j, k].rearrange("p a s -> p (a s)"), start=False,
                                                   stop=False, skip_group_check=True)
                                mm.then_inc(ev("placed"), 1)
                        pe.matmul(o, zeros[:, 0:P], zeros[:, :], start=False, stop=True,
                                  skip_group_check=True).then_inc(ev("placed_all"), 1)
                        for n in range(NT):
                            if n % 4 == 0:
                                pe.wait_ge(ev("gT"), n // 4 + 1)
                            if n >= 2:
                                pe.wait_ge(ev("first"), n - 1)
                            pe.matmul(bank[5 + n % 2][:, 0:H], gT[:, n * P:(n + 1) * P], b2r[:, :], start=True,
                                      stop=True).then_inc(ev("bias_product"), 1)

                    @block.sync
                    def _(sp):
                        sp.wait_ge(ev("zeroed"), 3)
                        sp.dma_start(sums[m][0][T:T + P, :], zero_sum[:, :]).then_inc(ev("sums_zeroed"), 16)
                        with sp.Fori(0, NT + 1) as i:
                            sp.dma_start(sums[m][1][bass.ds(i * P, P), :], zero_sum[:, :])\
                              .then_inc(ev("sums_zeroed"), 16)
                        with sp.Fori(0, NT // 2) as i:
                            for j in range(2):
                                n = i * 2 + j
                                sp.wait_ge(ev("first"), n + 1)
                                sp.dma_start(sums[m][0][bass.ds(n * P, P), :], first[:, j, :])\
                                  .then_inc(first_stored[j], 16)
                        sp.wait_ge(ev("sums_zeroed"), 16 * (NT + 2))
                        for j in range(2):
                            sp.wait_ge(first_stored[j], 16 * NT // 2)

        def experts(m, b1s, gather_at, add_at, gate_at, expert_at):
            with ExitStack() as own:
                def tmp(name, shape, dt=f32):
                    return own.enter_context(nc.sbuf_tensor(f"{name}_x{m}", shape, dt))
                ev = lambda name: sem(f"{name}_{m}")
                NG = 4
                gidx = tmp("gidx", [P, NG, 1], u32)
                aidx = tmp("aidx", [P, 2, 1], u32)
                rows = tmp("rows", [P, NG, 2 * H], f16)
                rT = tmp("rT", [P, 2, 4, P], f16)
                a = tmp("a", [P, 2, INNER])
                b = tmp("b", [P, 2, INNER])
                p = tmp("p", [P, 2, INNER])
                h = tmp("h", [P, 2, INNER])
                hs = tmp("hs", [P, 2, 4, P], f16)
                hT = tmp("hT", [P, 2, 4, P], f16)
                y = tmp("y", [P, 2, H])
                gathered = [ev(f"gathered{j}") for j in range(NG)]
                added = [ev(f"added{j}") for j in range(2)]
                PRODUCTS = ((0, 0), (0, 1), (1, 0))

                def there(s, lag):
                    return not isinstance(s, int) or 0 <= s + lag < SLOTS

                with nc.Block() as block:
                    @block.gpsimd
                    def _(pool):
                        def gather(n, c):
                            if later(n, NG):
                                pool.wait_ge(ev("turned"), n - (NG - 1))
                            pool.tensor_copy(gidx[:, c, :], gather_at[:, bass.ds(n, 1)]).then_inc(ev("gidx"), 1)
                            pool.wait_ge(ev("gidx"), n + 1)
                            hold(pool)
                            pool.indirect_dma_start(rows[:, c, :], None, t_rows[m],
                                                    bass.IndirectOffsetOnAxis(ap=gidx[:, c, :], axis=0))\
                                .then_inc(gathered[c], 16)

                        def add(n, c, past):
                            if later(n, 2):
                                pool.wait_ge(added[c % 2], past * 16)
                            pool.tensor_copy(aidx[:, c % 2, :], add_at[:, bass.ds(n, 1)]).then_inc(ev("aidx"), 1)
                            pool.wait_ge(ev("y"), n + 1)
                            pool.wait_ge(ev("aidx"), n + 1)
                            hold(pool)
                            pool.indirect_dma_start(sums[m][c % 2],
                                                    bass.IndirectOffsetOnAxis(ap=aidx[:, c % 2, :], axis=0),
                                                    y[:, c % 2, :], None, compute_op=ALU.add)\
                                .then_inc(added[c % 2], 16)

                        for n in range(NG):
                            gather(n, n)
                        for n in range(4, 6):
                            gather(n, n % 4)
                        for n in range(4):
                            add(n, n, n // 2)
                            gather(n + 6, (n + 6) % 4)
                        with pool.Fori(1, (SLOTS - 8) // 4) as i:
                            for c in range(4):
                                add(i * 4 + c, c, i * 2 + c // 2)
                                gather(i * 4 + (c + 6), (c + 6) % 4)
                        for n in range(SLOTS - 8, SLOTS):
                            add(n, n % 4, n // 2)
                            if n + 6 < SLOTS:
                                gather(n + 6, (n + 6) % 4)
                        for j in range(2):
                            pool.wait_ge(added[j], 16 * SLOTS // 2)

                    @block.tensor
                    def _(pe):
                        def turn_rows(n, c, nth):
                            pe.wait_ge(gathered[c], nth * 16 + 16)
                            if later(n, 2):
                                pe.wait_ge(ev("rT"), n - 1)
                            for q in range(4):
                                mm = pe.transpose(bank16[c % 2][:, q * P:(q + 1) * P], rows[:, c, q * P:(q + 1) * P],
                                                  ident16[:, :])
                            mm.then_inc(ev("turned"), 1)

                        def expert(n):
                            return pe.value_load(expert_at[0:1, bass.ds(n, 1)], min_val=0, max_val=E - 1)

                        def up(n, c):
                            e = bass.ds(expert(n), 1)
                            pe.wait_ge(ev("rT"), n + 1)
                            if later(n, 2):
                                pe.wait_ge(ev("a"), n - 1)
                                pe.wait_ge(ev("b"), n - 1)
                            o = bank[2 + c % 2][:, :]
                            pe.matmul(o, ones16[:, :], b1s[:, e, :], start=True, stop=False)
                            for k in range(HC):
                                for r, w in PRODUCTS:
                                    mm = pe.matmul(o, rT[:, c % 2, 2 * r + k, :], w1s[:, e, k, w, :], start=False,
                                                   stop=(k == HC - 1 and r == 1))
                            mm.then_inc(ev("up"), 1)

                        def turn_h(n, c):
                            pe.wait_ge(ev("h_lo"), n + 1)
                            if later(n, 2):
                                pe.wait_ge(ev("hT"), n - 1)
                            for q in range(4):
                                mm = pe.transpose(bank16[4 + c % 2][:, q * P:(q + 1) * P], hs[:, c % 2, q, :],
                                                  ident16[:, :])
                            mm.then_inc(ev("h_turned"), 1)

                        def down(n, c):
                            e = bass.ds(expert(n), 1)
                            pe.wait_ge(ev("hT"), n + 1)
                            if later(n, 2):
                                pe.wait_ge(ev("y"), n - 1)
                            o = bank[6 + c % 2][:, 0:H]
                            for k in range(2):
                                for r, w in PRODUCTS:
                                    mm = pe.matmul(o, hT[:, c % 2, 2 * r + k, :], w2s[:, e, k, w, :],
                                                   start=(k == 0 and r == 0 and w == 0), stop=(k == 1 and r == 1))
                            mm.then_inc(ev("down"), 1)

                        def emit(s, c, nth):
                            if there(s, 1):
                                turn_rows(s + 1, (c + 1) % 4, nth)
                            if there(s, 0):
                                up(s, c)
                            if there(s, -2):
                                down(s - 2, (c - 2) % 4)
                            if there(s, -1):
                                turn_h(s - 1, (c - 1) % 4)

                        for s in range(-1, 4):
                            emit(s, s % 4, (s + 1) // 4)
                        with pe.Fori(1, (SLOTS - 4) // 4) as i:
                            for q in range(4):
                                emit(i * 4 + q, q, i + (q + 1) // 4)
                        for s in range(SLOTS - 4, SLOTS + 2):
                            emit(s, s % 4, (s + 1) // 4)

                    @block.scalar
                    def _(act):
                        def rows_out(n, c):
                            act.wait_ge(ev("turned"), n + 1)
                            if later(n, 2):
                                act.wait_ge(ev("up"), n - 1)
                            act.activation(rT[:, c % 2], bank16[c % 2][:, 0:512].rearrange("p (q n) -> p q n", q=4),
                                           ACT.Copy).then_inc(ev("rT"), 1)

                        def gelu(n, c):
                            act.wait_ge(ev("a"), n + 1)
                            if later(n, 2):
                                act.wait_ge(ev("h"), n - 1)
                            act.activation(p[:, c % 2, :], a[:, c % 2, :], ACT.Gelu_apprx_sigmoid, scale=1.0 / S)\
                               .then_inc(ev("p"), 1)

                        def h_hi(n, c):
                            act.wait_ge(ev("h"), n + 1)
                            if later(n, 2):
                                act.wait_ge(ev("h_turned"), n - 1)
                            act.activation(hs[:, c % 2, 0:2, :], h[:, c % 2, :].rearrange("p (k n) -> p k n", k=2),
                                           ACT.Copy).then_inc(ev("h_hi"), 1)

                        def y_out(n, c, past):
                            act.wait_ge(ev("down"), n + 1)
                            if later(n, 2):
                                act.wait_ge(added[c % 2], past * 16)
                            act.activation(y[:, c % 2, :], bank[6 + c % 2][:, 0:H], ACT.Copy,
                                           scale=gate_at[:, bass.ds(n, 1)]).then_inc(ev("y"), 1)

                        def emit(s, c, past):
                            if there(s, 0):
                                gelu(s, c)
                            if there(s, -2):
                                y_out(s - 2, (c - 2) % 4, past)
                            if there(s, 0):
                                h_hi(s, c)
                            if there(s, 2):
                                rows_out(s + 2, (c + 2) % 4)

                        for s in range(-2, 4):
                            emit(s, s % 4, (s - 2) // 2)
                        with act.Fori(1, (SLOTS - 4) // 4) as i:
                            for q in range(4):
                                emit(i * 4 + q, q, i * 2 + (q - 2) // 2)
                        for s in range(SLOTS - 4, SLOTS + 2):
                            emit(s, s % 4, (s - 2) // 2)

                    @block.vector
                    def _(dve):
                        def clip_a(n, c):
                            dve.wait_ge(ev("up"), n + 1)
                            if later(n, 2):
                                dve.wait_ge(ev("p"), n - 1)
                            dve.tensor_scalar(a[:, c % 2, :], bank[2 + c % 2][:, 0:INNER], LIMIT * S, None, ALU.min)\
                               .then_inc(ev("a"), 1)

                        def clip_b(n, c):
                            if later(n, 2):
                                dve.wait_ge(ev("h"), n - 1)
                            dve.tensor_scalar(b[:, c % 2, :], bank[2 + c % 2][:, INNER:], LIMIT * S, -LIMIT * S,
                                              ALU.min, ALU.max).then_inc(ev("b"), 1)

                        def h_out(n, c):
                            dve.wait_ge(ev("b"), n + 1)
                            dve.wait_ge(ev("p"), n + 1)
                            if later(n, 2):
                                dve.wait_ge(ev("h_lo"), n - 1)
                            dve.scalar_tensor_tensor(h[:, c % 2, :], b[:, c % 2, :], S, p[:, c % 2, :], ALU.add,
                                                     ALU.mult).then_inc(ev("h"), 1)

                        def h_lo(n, c):
                            dve.wait_ge(ev("h_hi"), n + 1)
                            dve.tensor_tensor(hs[:, c % 2, 2:4, :], h[:, c % 2, :].rearrange("p (k n) -> p k n", k=2),
                                              hs[:, c % 2, 0:2, :], ALU.subtract).then_inc(ev("h_lo"), 1)

                        def hT_out(n, c):
                            dve.wait_ge(ev("h_turned"), n + 1)
                            if later(n, 2):
                                dve.wait_ge(ev("down"), n - 1)
                            dve.tensor_copy(hT[:, c % 2], bank16[4 + c % 2][:, 0:512].rearrange("p (q n) -> p q n", q=4))\
                               .then_inc(ev("hT"), 1)

                        def emit(s, c):
                            if there(s, 0):
                                clip_a(s, c)
                                clip_b(s, c)
                            if there(s, -1):
                                hT_out(s - 1, (c - 1) % 4)
                            if there(s, 0):
                                h_out(s, c)
                                h_lo(s, c)

                        for s in range(0, 4):
                            emit(s, s % 4)
                        with dve.Fori(1, (SLOTS - 4) // 4) as i:
                            for q in range(4):
                                emit(i * 4 + q, q)
                        for s in range(SLOTS - 4, SLOTS + 1):
                            emit(s, s % 4)

        def combine(m):
            with ExitStack() as own:
                ev = lambda name: sem(f"{name}_{m}")
                s01 = [[own.enter_context(nc.sbuf_tensor(f"sum{j}_{c}_{m}", [P, TPB, H], f32)) for j in range(2)]
                       for c in range(2)]
                back = [ev("sums_loaded0"), ev("sums_loaded1")]
                X4 = X[:, :, :].rearrange("p (b t) h -> p b t h", t=TPB)
                block = own.enter_context(nc.Block())

                @block.sync
                def _(sp):
                    with sp.Fori(0, B // 2) as i:
                        for c in range(2):
                            n = i * 2 + c
                            for j in range(2):
                                sp.dma_start(s01[c][j][:, :, :], sums[m][j][bass.ds(n * SEQ, SEQ), :]
                                             .rearrange("(t p) h -> p t h", p=P)).then_inc(back[c], 16)
                        sp.wait_ge(ev("combined"), i * 2 + 2)
                        hold(sp)
                    if m == 1:
                        for n in range(B):
                            sp.wait_ge(ev("combined"), n + 1)
                            sp.dma_start(out[n * SEQ:(n + 1) * SEQ, :].rearrange("(t p) h -> p t h", p=P),
                                         X[:, n * TPB:(n + 1) * TPB, :]).then_inc(ev("out_stored"), 16)
                        sp.wait_ge(ev("out_stored"), 16 * B)

                @block.vector
                def _(dve):
                    with dve.Fori(0, B // 2) as i:
                        for c in range(2):
                            n = i * 2 + c
                            dve.wait_ge(back[c], i * 32 + 32)
                            Xn = X4[:, bass.ds(n, 1)]
                            u, v = (s01[c][j][:, :, :].rearrange("p (o t) h -> p o t h", o=1) for j in range(2))
                            dve.tensor_tensor(u, u, v, ALU.add).then_inc(ev("summed"), 1)
                            dve.wait_ge(ev("summed"), n + 1)
                            dve.scalar_tensor_tensor(Xn, u, 0.5, Xn, ALU.mult, ALU.add).then_inc(ev("combined"), 1)

        def attention():
            with ExitStack() as own:
                def tmp(name, shape, dt=f32, where=own):
                    return where.enter_context(nc.sbuf_tensor(name, shape, dt))
                qk_dram = nc.dram_tensor("qk_split", (B, 2, 2, HEADS, D, SEQ), f16, kind="Internal").ap()
                stacks = [tmp(f"{n}_stack", [P, HEADS, SEQ], f16) for n in ("q", "k")]
                DV = D + 1
                v = tmp("v", [P, NT, HEADS, DV])
                bos = tmp("bos", [P, H])
                s = lambda name: sem(f"att_{name}")
                stack_loaded = [s(f"stack_loaded{g}") for g in range(QG)]
                PARTS = ((0, 0, 1), (0, 1, 0))

                def load_stacks(sp, b, g):
                    for c in range(2):
                        for r in range(3):
                            src = qk_dram[bass.ds(b, 1), c, PARTS[c][r], g * HG:(g + 1) * HG]
                            sp.dma_start(stacks[c][r * D:(r + 1) * D, g * HG:(g + 1) * HG, :],
                                         src.rearrange("o h d n -> d (o h) n")).then_inc(stack_loaded[g], 16)

                with ExitStack() as mine:
                    part = lambda name, shape, dt=f32: tmp(name, shape, dt, mine)
                    w_flat = part("w_raw", [P, HC * 3 * H])
                    w_raw = w_flat[:, :].rearrange("p (k n) -> p k n", k=HC)
                    w16 = part("w16", [P, 2, HC, 3 * H], f16)
                    bqk = part("bqk", [P, 4])
                    bvs = part("bvs", [P, H])
                    stats = part("stats_a", [P, NT, 6])
                    mv = part("mv_a", [P, NT, 2])
                    rz, shifted, root, newton = (part(f"{n}_a", [P, NT]) for n in ("rz", "shifted", "root", "newton"))
                    z = part("z_a", [P, TPB, H])
                    zT = part("zT", [P, 2, HC, SEQ], f16)
                    value = w_flat[:, 0:2 * SEQ].rearrange("p (a n) -> p a n", a=2)
                    hi = w_flat[:, 2 * SEQ:].bitcast(f16).rearrange("p (a n) -> p a n", a=2)
                    lo = part("qk_lo", [P, 2, SEQ], f16)
                    stored = [s("qk_stored0"), s("qk_stored1")]
                    block = mine.enter_context(nc.Block())
                    X4 = X[:, :, :].rearrange("p (b t) h -> p b t h", t=TPB)

                    @block.sync
                    def _(sp):
                        sp.dma_start(w_raw, wqkv).then_inc(s("w_loaded"), 16)
                        for dst, src in ((bqk[:, :], bias_qk), (bvs[:, :], spread(bv)), (bos[:, :], spread(bo))):
                            sp.dma_start(dst, src).then_inc(s("loaded"), 16)
                        sp.wait_ge(s("stacks_zeroed"), 2)
                        R = key_rows.shape[0]
                        for stack, src in zip(stacks, (query_rows, key_rows)):
                            sp.dma_start(stack[3 * D:3 * D + R, :, :], src).then_inc(s("loaded"), 16)
                        def emit(b):
                            for n in range(4):
                                c, g = n // 2, n % 2
                                for part_, tile, ready in ((0, hi, s("qk_hi")), (1, lo, s("qk_lo"))):
                                    sp.wait_ge(ready, b * 4 + n + 1)
                                    sp.dma_start(qk_dram[bass.ds(b, 1), c, part_, g * 8:(g + 1) * 8]
                                                 .rearrange("o h d n -> (o h d) n"), tile[:, n % 2, :])\
                                      .then_inc(stored[n % 2], 16)
                            if isinstance(b, int):
                                for j in range(2):
                                    sp.wait_ge(stored[j], 64)
                                for g in range(QG):
                                    load_stacks(sp, 0, g)
                        rounds(sp, B, emit)
                        for j in range(2):
                            sp.wait_ge(stored[j], B * 64)
                        sp.wait_ge(s("loaded"), 16 * 5)

                    @block.gpsimd
                    def _(pool):
                        for stack in stacks:
                            pool.memset(stack[:, :, :], 0.0).then_inc(s("stacks_zeroed"), 1)
                        pool.wait_ge(s("loaded"), 16 * 5)
                        def emit(b):
                            for n in range(4):
                                if later(b * 4 + n, 2) if isinstance(b, int) else True:
                                    pool.wait_ge(stored[n % 2], b * 64 + n // 2 * 32)
                                pool.wait_ge(s("qk_hi"), b * 4 + n + 1)
                                hold(pool)
                                pool.tensor_tensor(lo[:, n % 2, :], value[:, n % 2, :], hi[:, n % 2, :], ALU.subtract)\
                                    .then_inc(s("qk_lo"), 1)
                            pool.wait_ge(s("z"), b * TPB + TPB)
                            for t in range(TPB):
                                Xt = X4[:, bass.ds(b, 1), t]
                                pool.tensor_tensor(Xt, Xt, bos[:, :].rearrange("p (o h) -> p o h", o=1), ALU.add)
                        rounds(pool, B, emit)

                    @block.vector
                    def _(dve):
                        for i in range(NT):
                            dve.bn_stats(stats[:, i, :], X[:, i, :]).then_inc(s("stats"), 1)
                        for i in range(NT):
                            dve.wait_ge(s("stats"), i + 1)
                            dve.bn_aggr(mv[:, i, :], stats[:, i, :]).then_inc(s("moments"), 1)
                        dve.wait_ge(s("moments"), NT)
                        rsqrt(dve, chained(dve, s("rz_steps")), rz[:, :], mv[:, :, 1], shifted[:, :], root[:, :],
                              newton[:, :], s("to_root"), s("rooted"), 1)
                        dve.memset(v[:, :, :, D:], 1.0).then_inc(s("ones"), 1)
                        for o in (4, 5):
                            dve.memset(bank[o][:, :], 1.0).then_inc(s("banks_filled"), 1)
                        dve.wait_ge(s("w_hi"), 1)
                        dve.scalar_tensor_tensor(w16[:, 1], w_raw, WS, w16[:, 0], ALU.mult, ALU.subtract)\
                           .then_inc(s("w_lo"), 1)
                        dve.wait_ge(s("loaded"), 16 * 5)
                        def emit(b):
                            if later(b, 1):
                                dve.wait_ge(s("z_turned"), b * HC)
                            for t in range(TPB):
                                one = bass.ds(b * TPB + t, 1)
                                dve.tensor_scalar(z[:, t:t + 1, :], X[:, one, :], mv[:, one, 0], rz[:, one],
                                                  ALU.subtract, ALU.mult).then_inc(s("z"), 1)
                            for k in range(HC):
                                dve.wait_ge(s("zT_hi"), b * HC + k + 1)
                                dve.tensor_tensor(zT[:, 1, k, :], bank[k][:, :], zT[:, 0, k, :], ALU.subtract)\
                                   .then_inc(s("zT_lo"), 1)
                            for n in range(4):
                                dve.wait_ge(s("qk_product"), b * 4 + n + 1)
                                if later(b, 1) or n >= 2:
                                    dve.wait_ge(s("qk_lo"), b * 4 + n - 1)
                                    hold(dve)
                                dve.tensor_scalar(value[:, n % 2, :], bank[2 + n % 2][:, :], 1.0 / WS, bqk[:, n:n + 1],
                                                  ALU.mult, ALU.add).then_inc(s("value"), 1)
                            for t in range(TPB):
                                dve.wait_ge(s("v_product"), b * TPB + t + 1)
                                dve.scalar_tensor_tensor(
                                    v[:, bass.ds(b * TPB + t, 1), :, 0:D],
                                    bank[6 + t % 2][:, 0:H].rearrange("p (o h d) -> p o h d", o=1, d=D), 1.0 / WS,
                                    bvs[:, :].rearrange("p (o h d) -> p o h d", o=1, d=D), ALU.mult, ALU.add)\
                                   .then_inc(s("v"), 1)
                        rounds(dve, B, emit)

                    @block.scalar
                    def _(act):
                        act.wait_ge(s("to_root"), 1)
                        act.activation(root[:, :], shifted[:, :], ACT.Sqrt).then_inc(s("rooted"), 1)
                        act.wait_ge(s("w_loaded"), 16)
                        act.activation(w16[:, 0], w_raw, ACT.Copy, scale=WS).then_inc(s("w_hi"), 1)
                        def emit(b):
                            for k in range(HC):
                                act.wait_ge(s("z_turned"), b * HC + k + 1)
                                act.activation(zT[:, 0, k, :], bank[k][:, :], ACT.Copy).then_inc(s("zT_hi"), 1)
                            for n in range(4):
                                if later(b, 1) or n >= 2:
                                    act.wait_ge(stored[n % 2], b * 64 + n // 2 * 32)
                                act.wait_ge(s("value"), b * 4 + n + 1)
                                act.activation(hi[:, n % 2, :], value[:, n % 2, :], ACT.Copy).then_inc(s("qk_hi"), 1)
                        rounds(act, B, emit)

                    @block.tensor
                    def _(pe):
                        PRODUCTS = ((0, 0), (0, 1), (1, 0))
                        def emit(b):
                            for k in range(HC):
                                if k == 0 and later(b, 1):
                                    pe.wait_ge(s("zT_lo"), b * HC)
                                for t in range(TPB):
                                    if k == 0:
                                        pe.wait_ge(s("z"), b * TPB + t + 1)
                                    mm = pe.transpose(bank[k][:, t * P:(t + 1) * P], z[:, t, k * P:(k + 1) * P],
                                                      ident[:, :])
                                mm.then_inc(s("z_turned"), 1)
                            if isinstance(b, int):
                                pe.wait_ge(s("w_lo"), 1)
                            for n in range(4):
                                if later(b, 1) or n >= 2:
                                    pe.wait_ge(s("value"), b * 4 + n - 1)
                                if n == 0:
                                    pe.wait_ge(s("zT_lo"), b * HC + HC)
                                for k in range(HC):
                                    for r, w in PRODUCTS:
                                        mm = pe.matmul(bank[2 + n % 2][:, :], w16[:, w, k, n * P:(n + 1) * P],
                                                       zT[:, r, k, :], start=(k == 0 and r == 0 and w == 0),
                                                       stop=(k == HC - 1 and r == 1))
                                mm.then_inc(s("qk_product"), 1)
                            for t in range(TPB):
                                if later(b, 1) or t >= 2:
                                    pe.wait_ge(s("v"), b * TPB + t - 1)
                                for k in range(HC):
                                    for r, w in PRODUCTS:
                                        mm = pe.matmul(bank[6 + t % 2][:, 0:H], zT[:, r, k, t * P:(t + 1) * P],
                                                       w16[:, w, k, 2 * H:], start=(k == 0 and r == 0 and w == 0),
                                                       stop=(k == HC - 1 and r == 1))
                                mm.then_inc(s("v_product"), 1)
                        rounds(pe, B, emit)

                probs = tmp("probs", [P, 2, HG, SEQ])
                mx = tmp("mx", [P, 2, TPB, HG])
                wos = tmp("wos", [P, QG, H])
                maskq = tmp("maskq", [P, P], bf16)
                maskk = tmp("maskk", [P, P], bf16)
                identb = tmp("identb", [P, P], bf16)
                minus = tmp("minus", [P, HG, P], bf16)
                spread_sum = tmp("spread_sum", [P, P])
                maxT = tmp("maxT", [P, 2, SEQ], bf16)
                v_near = tmp("v_near", [P, 2, TPB, HG, DV])
                oT = tmp("oT", [P, QG, SEQ])
                re = tmp("re", [P, SEQ])
                U = HG * TPB
                by_query = lambda k: (k // TPB, k % TPB)
                by_key = lambda k: (k // HG, k % HG)
                ahead = {k: [u for u in range(U) if u * 12 // U == k] for k in range(U)}

                def batches(eng, emit):
                    emit(0)
                    with eng.Fori(1, B - 1) as b:
                        emit(b)
                    emit(B - 1)

                def follows(b, g):
                    return not isinstance(b, int) or b * QG + g + 1 < B * QG

                with nc.Block() as block:
                    @block.gpsimd
                    def _(pool):
                        made = s("tables")
                        for tile in (maskq, maskk, identb, minus, spread_sum, maxT):
                            pool.memset(tile[:], 0.0).then_inc(made, 1)
                        pool.wait_ge(made, 6)
                        pool.affine_select(maskq[:, :], maskq[:, :], [[-1, P]], ALU.is_ge, MASKED, 0, 1).then_inc(made, 1)
                        pool.affine_select(maskk[:, :], maskk[:, :], [[1, P]], ALU.is_ge, MASKED, 0, -1).then_inc(made, 1)
                        pool.affine_select(identb[:, :], identb[:, :], [[-1, P]], ALU.not_equal, 1.0, 0, 1)\
                            .then_inc(made, 1)
                        pool.affine_select(minus[:, :, :], minus[:, :, :], [[-1, HG], [0, P]], ALU.not_equal, -1.0, 0, 1)\
                            .then_inc(made, 1)
                        pool.affine_select(spread_sum[:, :].rearrange("p (c r) -> p c r", r=32),
                                           spread_sum[:, :].rearrange("p (c r) -> p c r", r=32),
                                           [[-32, HG], [0, 32]], ALU.not_equal, 1.0, -D, 1).then_inc(made, 1)
                        def emit(b):
                            for g in range(QG):
                                n = b * QG + g
                                if later(n, 2):
                                    pool.wait_ge(s("weighed"), (n - 1) * TPB)
                                pool.tensor_copy(v_near[:, g % 2].rearrange("p (o t) h d -> p o t h d", o=1),
                                                 v[:, :, g * HG:(g + 1) * HG, :]
                                                 .rearrange("p (b t) h d -> p b t h d", t=TPB)[:, bass.ds(b, 1)])\
                                    .then_inc(s("v_near"), 1)
                        rounds(pool, B, emit)

                    @block.sync
                    def _(sp):
                        sp.dma_start(wos[:, :, :], wo).then_inc(s("wo_loaded"), 16)
                        with sp.Fori(1, B) as b:
                            for g in range(QG):
                                sp.wait_ge(s("scores_k"), ((b - 1) * QG + g + 1) * U)
                                hold(sp)
                                load_stacks(sp, b, g)
                        for g in range(QG):
                            sp.wait_ge(stack_loaded[g], B * 96)

                    @block.tensor
                    def _(pe):
                        def score_q(b, g, u):
                            n = b * QG + g
                            c, i = by_query(u)
                            h = g * HG + c
                            if u == 0:
                                pe.wait_ge(stack_loaded[g], b * 96 + 96)
                            if later(n, 1) or u >= 2:
                                pe.wait_ge(s("max"), n * U + u - 1)
                            o = bank[u % 2]
                            pe.matmul(o[:, 0:(i + 1) * P], stacks[0][:, h, i * P:(i + 1) * P],
                                      stacks[1][:, h, 0:(i + 1) * P], start=True, stop=False, skip_group_check=True)
                            pe.matmul(o[:, i * P:(i + 1) * P], identb[:, :], maskq[:, :], start=False, stop=True,
                                      skip_group_check=True).then_inc(s("scores_q"), 1)

                        def turn_max(n, g):
                            pe.wait_ge(s("max"), n * U + U)
                            for i in range(TPB):
                                mm = pe.transpose(bank[6][0:HG, i * P:(i + 1) * P], mx[:, g % 2, i, :], ident[:, :])
                            mm.then_inc(s("max_turned"), 1)

                        def score_k(n, g, u):
                            j, c = by_key(u)
                            h, W = g * HG + c, SEQ - j * P
                            if u == 0:
                                pe.wait_ge(s("maxT"), n + 1)
                            if later(n, 1) or u >= 2:
                                pe.wait_ge(s("exp"), n * U + u - 1)
                            o = bank[2 + u % 2]
                            pe.matmul(o[:, 0:W], stacks[1][:, h, j * P:(j + 1) * P], stacks[0][:, h, j * P:],
                                      start=True, stop=False, skip_group_check=True)
                            pe.matmul(o[:, 0:W], minus[:, c, :], maxT[:, g % 2, j * P:], start=False, stop=False,
                                      skip_group_check=True)
                            pe.matmul(o[:, 0:P], identb[:, :], maskk[:, :], start=False, stop=True,
                                      skip_group_check=True).then_inc(s("scores_k"), 1)

                        def weigh(b, n, g, j):
                            if j == 0:
                                pe.wait_ge(s("v_near"), n + 1)
                            pe.wait_ge(s("exp"), n * U + (j + 1) * HG)
                            if j == 0 and later(n, 2):
                                pe.wait_ge(s("o_copied"), n - 1)
                            for c in range(HG):
                                mm = pe.matmul(bank[4 + g % 2][32 * c:32 * c + DV, j * P:],
                                               v_near[:, g % 2, j, c, :],
                                               probs[:, j % 2, c, 0:SEQ - j * P], start=(j == 0), stop=(j == TPB - 1),
                                               tile_position=(0, 32 * c), skip_group_check=True)
                            mm.then_inc(s("weighed"), 1)

                        def spread_sums(b, g):
                            n = b * QG + g
                            pe.wait_ge(s("o_copied"), n + 1)
                            if later(n, 1):
                                pe.wait_ge(s("re"), n * 4)
                            if g == 0 and later(b, 1):
                                pe.wait_ge(s("x"), b * 2)
                            pe.matmul(bank[7][:, :], spread_sum[:, :], oT[:, g, :], start=True, stop=True)\
                              .then_inc(s("sums_spread"), 1)

                        def project_out(b, pair):
                            pe.wait_ge(s("wo_loaded"), 16)
                            pe.wait_ge(s("oT"), b * QG + QG)
                            if pair:
                                pe.wait_ge(s("x"), b * 2 + 1)
                            for t in (2 * pair, 2 * pair + 1):
                                for g in range(QG):
                                    mm = pe.matmul(bank[7][:, t % 2 * H:(t % 2 + 1) * H], oT[:, g, t * P:(t + 1) * P],
                                                   wos[:, g, :], start=(g == 0), stop=(g == QG - 1),
                                                   skip_group_check=True)
                            mm.then_inc(s("out_product"), 1)

                        def emit(b):
                            for g in range(QG):
                                n = b * QG + g
                                if g == 0 and isinstance(b, int) and b == 0:
                                    pe.wait_ge(s("tables"), 11)
                                    for u in range(U):
                                        score_q(b, 0, u)
                                    turn_max(n, g)
                                for k in range(U):
                                    score_k(n, g, k)
                                    if follows(b, g):
                                        for u in ahead[k]:
                                            score_q(b + (g + 1) // QG, (g + 1) % QG, u)
                                        if k == 14:
                                            turn_max(n + 1, (g + 1) % QG)
                                    if k in (5, 9, 13):
                                        weigh(b, n, g, (k - 5) // 4)
                                    if later(n, 1):
                                        bp = b if g else b - 1
                                        if k == 1:
                                            weigh(bp, n - 1, (g - 1) % QG, TPB - 1)
                                        if k == 4:
                                            spread_sums(bp, (g - 1) % QG)
                                        if k in (11, 14) and g == 0:
                                            project_out(bp, (k - 11) // 3)
                            if isinstance(b, int) and b == B - 1:
                                weigh(b, n, g, TPB - 1)
                                spread_sums(b, g)
                                for pair in range(2):
                                    project_out(b, pair)
                        batches(pe, emit)

                    @block.scalar
                    def _(act):
                        def rows_of_max(n, g):
                            act.wait_ge(s("max_turned"), n + 1)
                            act.activation(maxT[0:HG, g % 2, :], bank[6][0:HG, :], ACT.Copy).then_inc(s("maxT"), 1)

                        def copy_o(b, g):
                            act.wait_ge(s("weighed"), (b * QG + g) * TPB + TPB)
                            if g == 0 and later(b, 1):
                                act.wait_ge(s("out_product"), b * 2)
                            act.activation(oT[:, g, :], bank[4 + g % 2][:, :], ACT.Copy).then_inc(s("o_copied"), 1)

                        def emit(b):
                            for g in range(QG):
                                n = b * QG + g
                                if g == 0 and isinstance(b, int) and b == 0:
                                    act.wait_ge(s("tables"), 11)
                                    rows_of_max(n, g)
                                for k in range(U):
                                    j, c = by_key(k)
                                    act.wait_ge(s("scores_k"), n * U + k + 1)
                                    if c == 0 and (later(n, 1) or j >= 2):
                                        act.wait_ge(s("weighed"), n * TPB + j - 1)
                                    act.activation(probs[:, j % 2, c, 0:SEQ - j * P], bank[2 + k % 2][:, 0:SEQ - j * P],
                                                   ACT.Exp, scale=0.25).then_inc(s("exp"), 1)
                                    if k == 14 and follows(b, g):
                                        rows_of_max(n + 1, (g + 1) % QG)
                                    if k == 2 and later(n, 1):
                                        copy_o(b if g else b - 1, (g - 1) % QG)
                            if isinstance(b, int) and b == B - 1:
                                copy_o(b, g)
                        batches(act, emit)

                    @block.vector
                    def _(dve):
                        def take_max(n, g, u):
                            c, i = by_query(u)
                            dve.wait_ge(s("scores_q"), n * U + u + 1)
                            if u == 0 and later(n, 2):
                                dve.wait_ge(s("max_turned"), n - 1)
                            dve.tensor_reduce(mx[:, g % 2, i, c:c + 1], bank[u % 2][:, 0:(i + 1) * P], AX.X, ALU.max)\
                               .then_inc(s("max"), 1)

                        def invert(n, q):
                            if q == 0:
                                dve.wait_ge(s("sums_spread"), n + 1)
                                if later(n, 1):
                                    dve.wait_ge(s("oT"), n)
                            dve.reciprocal(re[:, q * P:(q + 1) * P], bank[7][:, q * P:(q + 1) * P])\
                               .then_inc(s("re"), 1)

                        def divide(n, g):
                            dve.wait_ge(s("re"), n * 4 + 4)
                            dve.tensor_tensor(oT[:, g, :], oT[:, g, :], re[:, :], ALU.mult).then_inc(s("oT"), 1)

                        def add_out(b, pair):
                            dve.wait_ge(s("out_product"), b * 2 + pair + 1)
                            Xt = X[:, bass.ds(b * TPB + 2 * pair, 2), :]
                            dve.tensor_tensor(Xt, Xt, bank[7][:, :].rearrange("p (t h) -> p t h", t=2), ALU.add)\
                               .then_inc(s("x"), 1)

                        def emit(b):
                            for g in range(QG):
                                n = b * QG + g
                                if g == 0 and isinstance(b, int) and b == 0:
                                    for u in range(U):
                                        take_max(0, 0, u)
                                for k in range(U):
                                    if follows(b, g):
                                        for u in ahead[k]:
                                            take_max(n + 1, (g + 1) % QG, u)
                                    if later(n, 1):
                                        if k in (5, 6, 7, 8):
                                            invert(n - 1, k - 5)
                                        if k == 9:
                                            divide(n - 1, (g - 1) % QG)
                                        if k in (12, 15) and g == 0:
                                            add_out(b - 1, (k - 12) // 3)
                            if isinstance(b, int) and b == B - 1:
                                for q in range(4):
                                    invert(n, q)
                                divide(n, g)
                                for pair in range(2):
                                    add_out(b, pair)
                        batches(dve, emit)

        def moe(m):
            with ExitStack() as own:
                tabs = [own.enter_context(nc.sbuf_tensor(f"{n}{m}", [P, SLOTS], dt))
                        for n, dt in (("gather_at", u32), ("add_at", u32), ("gate_at", f32), ("expert_at", i32))]
                b1s = own.enter_context(nc.sbuf_tensor(f"b1s{m}", [P, E, 2 * INNER], f16))
                route(m, b1s, *tabs)
                experts(m, b1s, *tabs)
            combine(m)

        setup()
        moe(0)
        end_phase()
        attention()
        end_phase()
        moe(1)
        end_phase()


def kernel(L0_attn_x, L0_attn_Wqkv, L0_attn_bqkv, L0_attn_Wo, L0_attn_bo, L0_ffn_norm_w, L0_ffn_gate_w,
           L0_ffn_gate_b, L0_ffn_w1, L0_ffn_b1, L0_ffn_w2, L0_ffn_b2):
    import numpy as np
    import concourse.bacc as bacc
    from concourse.bass_utils import run_bass_kernel_spmd

    def chunks(w):
        return w.reshape(-1, P, w.shape[-1]).transpose(1, 0, 2)

    def heads_at_32(w):
        wide = np.zeros((HEADS, 32, w.shape[1]), w.dtype)
        wide[:, 0:D] = w.reshape(HEADS, D, w.shape[1])
        return wide.reshape(HEADS * 32, w.shape[1])

    def parts(a):
        found = []
        for _ in range(3):
            found.append(a.astype(np.float16))
            a = a - found[-1]
        return found

    slopes = np.float32(2.0 ** (-np.arange(HEADS) / 2)).astype(np.float64)[:, None]
    place, start = np.arange(SEQ) % P, np.arange(SEQ) // P * P
    key_rows = parts(4 * slopes * (place - P // 2))
    query_rows = [np.ones((HEADS, SEQ), np.float16)] * 3
    for q in range(TPB):
        key_rows += parts(4 * slopes * (start - q * P))
        query_rows += [np.broadcast_to((start == q * P).astype(np.float16), (HEADS, SEQ))] * 3
    key_rows, query_rows = np.stack(key_rows), np.stack(query_rows)

    bqkv = np.asarray(L0_attn_bqkv)
    w1 = np.asarray(L0_ffn_w1).transpose(0, 2, 1)
    w1 = w1.reshape(E, H, INNER, 2).transpose(0, 1, 3, 2)
    w1 = w1.reshape(E, HC, P, 2 * INNER).transpose(0, 2, 1, 3)
    w2 = np.asarray(L0_ffn_w2).transpose(0, 2, 1).reshape(E, 2, P, H).transpose(0, 2, 1, 3)
    arrays = {
        "x": np.asarray(L0_attn_x).reshape(T, H),
        "wqkv": chunks(np.asarray(L0_attn_Wqkv)),
        "bias_qk": bqkv[0:2 * H].reshape(4, P).T,
        "bv": bqkv[2 * H:],
        "wo": chunks(heads_at_32(np.asarray(L0_attn_Wo))),
        "bo": np.asarray(L0_attn_bo),
        "query_rows": query_rows,
        "key_rows": key_rows,
        "norm_w": np.asarray(L0_ffn_norm_w),
        "gate_w": chunks(np.asarray(L0_ffn_gate_w).T),
        "gate_b": np.asarray(L0_ffn_gate_b),
        "w1": w1.reshape(E, P, HC * 2 * INNER),
        "b1": np.asarray(L0_ffn_b1).reshape(E, INNER, 2).transpose(0, 2, 1).reshape(E, 2 * INNER),
        "w2": w2.reshape(E, P, 2 * H),
        "b2": np.asarray(L0_ffn_b2),
    }
    nc = bacc.Bacc("TRN2", target_bir_lowering=False, num_devices=1)
    feeds, args = {}, []
    for name, a in arrays.items():
        a = np.ascontiguousarray(a)
        feeds[f"in_{name}"] = a
        args.append(nc.dram_tensor(f"in_{name}", a.shape, mybir.dt.from_np(a.dtype), kind="ExternalInput").ap())
    out = nc.dram_tensor("out", (T, H), f32, kind="ExternalOutput").ap()
    build(nc, *args, out)
    result = run_bass_kernel_spmd(nc, [feeds], core_ids=[0])
    return result.results[0]["out"].reshape(B, SEQ, H)
```
